# Optimizing a Trainium2 kernel written in Bass

```python
import numpy as np
import jax
import jax.numpy as jnp

def _softmax(x, axis=-1):
    return jax.nn.softmax(x, axis=axis)

def _gelu(x):
    return jax.nn.gelu(x, approximate=True)

def _silu(x):
    return jax.nn.silu(x)

def _sigmoid(x):
    return jax.nn.sigmoid(x)

def _layernorm(x, axis=-1, eps=1e-05):
    m = jnp.mean(x, axis=axis, keepdims=True)
    v = jnp.var(x, axis=axis, keepdims=True)
    return (x - m) / jnp.sqrt(v + eps)

def _scatter_add(tgt, idx, src, axis=0):
    return tgt.at[idx].add(src)

def _segment_sum(src, seg, n):
    return jax.ops.segment_sum(src, seg, n)
kernel_name = 'mk_flamingo_gated_d2_seqx_r8_022681'

def setup_inputs(seed: int=0):
    np.random.seed(seed)
    _w = jnp.asarray

    def _rec_inputs():
        import jax
        import jax.numpy as jnp
        _rk = jax.random.key(seed)
        x = 0.0002417 + 0.9998 * jax.random.normal(jax.random.fold_in(_rk, 1), (32, 64, 128), jnp.float32)
        _lenS = 64 - jax.random.randint(jax.random.fold_in(_rk, 7), (32,), 0, max(1, 64 // 4) + 1, jnp.int32)
        _lenS2 = 64 - jax.random.randint(jax.random.fold_in(_rk, 8), (32,), 0, max(1, 64 // 4) + 1, jnp.int32)
        _ctx_1024P = jax.random.normal(jax.random.fold_in(_rk, 11), (32, 16, 128), jnp.float32)
        _ctx_1024c = jax.random.dirichlet(jax.random.fold_in(_rk, 511), 0.3 * jnp.ones((16,), jnp.float32), (32, 64))
        _ctx_1024t = jnp.einsum('bsk,bkd->bsd', _ctx_1024c, _ctx_1024P)
        _ctx_1024t = _ctx_1024t * jax.lax.rsqrt(jnp.mean(jnp.square(_ctx_1024t)) + 1e-12) * 0.953939
        ctx_1024 = 7.22013e-05 + 1.00017 * (_ctx_1024t + 0.3 * jax.random.normal(jax.random.fold_in(_rk, 611), (32, 64, 128), jnp.float32))
        _g = jax.random.normal(jax.random.fold_in(_rk, 9001), (2, 2), jnp.float32)
        _g = jnp.sign(_g) * jnp.maximum(jnp.abs(_g), 1.0) + (_g == 0) * 1.0
        g_xattn = _g[0]
        g_ffn = _g[1]
        return (x, ctx_1024, g_xattn, g_ffn)
    x, ctx_1024, g_xattn, g_ffn = _rec_inputs()

    def _L0_xattn_setup():
        import jax, jax.numpy as jnp
        import numpy as np
        D_MODEL = 128
        B, S = (4, 256)
        key = jax.random.key(seed)
        ks = jax.random.split(key, 10)
        s = 1.0 / np.sqrt(D_MODEL)
        return {'k': jax.random.normal(ks[0], (B, S, D_MODEL), jnp.float32), 'v': jax.random.normal(ks[1], (B, S, D_MODEL), jnp.float32), 'q': jax.random.normal(ks[2], (B, S, D_MODEL), jnp.float32), 'Wk': jax.random.normal(ks[3], (D_MODEL, D_MODEL), jnp.float32) * s, 'Wv': jax.random.normal(ks[4], (D_MODEL, D_MODEL), jnp.float32) * s, 'bv': jnp.zeros((D_MODEL,), jnp.float32), 'Wq': jax.random.normal(ks[5], (D_MODEL, D_MODEL), jnp.float32) * s, 'bq': jnp.zeros((D_MODEL,), jnp.float32), 'Wo': jax.random.normal(ks[6], (D_MODEL, D_MODEL), jnp.float32) * s, 'bo': jnp.zeros((D_MODEL,), jnp.float32)}
    _L0_xattn_all = _L0_xattn_setup()
    _L0_xattn_in = {k: v for k, v in _L0_xattn_all.items() if k in ('Wk', 'Wv', 'bv', 'Wq', 'bq', 'Wo', 'bo')}
    del _L0_xattn_all

    def _L0_ffn_setup():
        import jax, jax.numpy as jnp
        import numpy as np
        B, S, D = (4, 256, 128)
        O = 128
        E = 8
        K = 2
        key = jax.random.key(seed)
        k1, k2, k3, k4, k5 = jax.random.split(key, 5)
        scale = 1.0 / np.sqrt(D)
        x = jax.random.normal(k1, (B, S, D), dtype=jnp.float32)
        We = jax.random.uniform(k2, (E, D, O), dtype=jnp.float32, minval=-scale, maxval=scale)
        be = jax.random.uniform(k3, (E, O), dtype=jnp.float32, minval=-scale, maxval=scale)
        Wg = jax.random.uniform(k4, (D, E), dtype=jnp.float32, minval=-scale, maxval=scale)
        bg = jax.random.uniform(k5, (E,), dtype=jnp.float32, minval=-scale, maxval=scale)
        return {'x': x, 'We': We, 'be': be, 'Wg': Wg, 'bg': bg}
    _L0_ffn_all = _L0_ffn_setup()
    _L0_ffn_in = {k: v for k, v in _L0_ffn_all.items() if k in ('We', 'be', 'Wg', 'bg')}
    del _L0_ffn_all

    def _L1_xattn_setup():
        import jax, jax.numpy as jnp
        import numpy as np
        N_EMBD = 128
        COND = 128
        N_HEAD = 16
        B, N, NTOK = (4, 256, 256)
        key = jax.random.key(seed)
        ks = jax.random.split(key, 10)
        s = 0.02
        return {'x': jax.random.normal(ks[0], (B, N, N_EMBD), jnp.float32), 'encoder_output': jax.random.normal(ks[1], (B, NTOK, COND), jnp.float32), 'Wq': jax.random.normal(ks[2], (N_EMBD, N_EMBD), jnp.float32) * s, 'bq': jnp.zeros((N_EMBD,), jnp.float32), 'Wk': jax.random.normal(ks[3], (N_EMBD, COND), jnp.float32) * s, 'bk': jnp.zeros((N_EMBD,), jnp.float32), 'Wv': jax.random.normal(ks[4], (N_EMBD, COND), jnp.float32) * s, 'bv': jnp.zeros((N_EMBD,), jnp.float32), 'Wp': jax.random.normal(ks[5], (N_EMBD, N_EMBD), jnp.float32) * s, 'bp': jnp.zeros((N_EMBD,), jnp.float32)}
    _L1_xattn_all = _L1_xattn_setup()
    _L1_xattn_in = {k: v for k, v in _L1_xattn_all.items() if k in ('Wq', 'bq', 'Wk', 'bk', 'Wv', 'bv', 'Wp', 'bp')}
    del _L1_xattn_all

    def _L1_ffn_setup():
        import jax, jax.numpy as jnp
        import numpy as np
        key = jax.random.key(seed)
        ks = jax.random.split(key, 5)
        B, T, D, E = (4, 256, 128, 8)
        inputs = jax.random.normal(ks[0], (B, T, D), dtype=jnp.float32)
        Wr = jax.random.normal(ks[1], (D, E), dtype=jnp.float32) * 0.02
        br = jnp.zeros((E,), dtype=jnp.float32)
        W1 = jax.random.normal(ks[2], (E, D, D), dtype=jnp.float32) * 0.02
        b1 = jnp.zeros((E, D), dtype=jnp.float32)
        W2 = jax.random.normal(ks[3], (E, D, D), dtype=jnp.float32) * 0.02
        b2 = jnp.zeros((E, D), dtype=jnp.float32)
        return {'inputs': inputs, 'Wr': Wr, 'br': br, 'W1': W1, 'b1': b1, 'W2': W2, 'b2': b2}
    _L1_ffn_all = _L1_ffn_setup()
    _L1_ffn_in = {k: v for k, v in _L1_ffn_all.items() if k in ('Wr', 'br', 'W1', 'b1', 'W2', 'b2')}
    del _L1_ffn_all
    return {'x': x, 'ctx_1024': ctx_1024, 'g_xattn': g_xattn, 'g_ffn': g_ffn, 'L0_xattn_Wk': _L0_xattn_in['Wk'], 'L0_xattn_Wv': _L0_xattn_in['Wv'], 'L0_xattn_bv': _L0_xattn_in['bv'], 'L0_xattn_Wq': _L0_xattn_in['Wq'], 'L0_xattn_bq': _L0_xattn_in['bq'], 'L0_xattn_Wo': _L0_xattn_in['Wo'], 'L0_xattn_bo': _L0_xattn_in['bo'], 'L0_ffn_We': _L0_ffn_in['We'], 'L0_ffn_be': _L0_ffn_in['be'], 'L0_ffn_Wg': _L0_ffn_in['Wg'], 'L0_ffn_bg': _L0_ffn_in['bg'], 'L1_xattn_Wq': _L1_xattn_in['Wq'], 'L1_xattn_bq': _L1_xattn_in['bq'], 'L1_xattn_Wk': _L1_xattn_in['Wk'], 'L1_xattn_bk': _L1_xattn_in['bk'], 'L1_xattn_Wv': _L1_xattn_in['Wv'], 'L1_xattn_bv': _L1_xattn_in['bv'], 'L1_xattn_Wp': _L1_xattn_in['Wp'], 'L1_xattn_bp': _L1_xattn_in['bp'], 'L1_ffn_Wr': _L1_ffn_in['Wr'], 'L1_ffn_br': _L1_ffn_in['br'], 'L1_ffn_W1': _L1_ffn_in['W1'], 'L1_ffn_b1': _L1_ffn_in['b1'], 'L1_ffn_W2': _L1_ffn_in['W2'], 'L1_ffn_b2': _L1_ffn_in['b2']}

def reference(x, ctx_1024, g_xattn, g_ffn, L0_xattn_Wk, L0_xattn_Wv, L0_xattn_bv, L0_xattn_Wq, L0_xattn_bq, L0_xattn_Wo, L0_xattn_bo, L0_ffn_We, L0_ffn_be, L0_ffn_Wg, L0_ffn_bg, L1_xattn_Wq, L1_xattn_bq, L1_xattn_Wk, L1_xattn_bk, L1_xattn_Wv, L1_xattn_bv, L1_xattn_Wp, L1_xattn_bp, L1_ffn_Wr, L1_ffn_br, L1_ffn_W1, L1_ffn_b1, L1_ffn_W2, L1_ffn_b2):
    import jax
    import jax.numpy as jnp

    def _L0_xattn_ref(k, v, q, Wk, Wv, bv, Wq, bq, Wo, bo):
        import jax, jax.numpy as jnp
        import numpy as np
        D_MODEL = 128
        B, S = (4, 256)
        kp = jnp.einsum('bsd,ed->bse', k, Wk)
        vp = jnp.einsum('bsd,ed->bse', v, Wv) + bv
        qp = jnp.einsum('bsd,ed->bse', q, Wq) + bq
        scale = 1.0 / jnp.sqrt(jnp.float32(kp.shape[-1]))
        scores = jnp.einsum('bqd,bkd->bqk', qp, kp) * scale
        probs = jax.nn.softmax(scores, axis=-1)
        ctx = jnp.einsum('bqk,bkd->bqd', probs, vp)
        return jnp.einsum('bqd,ed->bqe', ctx, Wo) + bo

    def _L0_ffn_ref(x, We, be, Wg, bg):
        import jax, jax.numpy as jnp
        import numpy as np
        B, S, D = (4, 256, 128)
        O = 128
        E = 8
        K = 2
        b, s, d = x.shape
        x_flat = x.reshape(-1, d)
        gates = jax.nn.softmax(x_flat @ Wg + bg, axis=-1)
        topk_gates, topk_idx = jax.lax.top_k(gates, K)
        topk_gates = topk_gates / jnp.sum(topk_gates, axis=1, keepdims=True)
        expert_out = jnp.einsum('nd,edo->neo', x_flat, We) + be
        selected = jnp.take_along_axis(expert_out, topk_idx[:, :, None], axis=1)
        out = jnp.sum(selected * topk_gates[:, :, None], axis=1)
        return out.reshape(b, s, -1)

    def _L1_xattn_ref(x, encoder_output, Wq, bq, Wk, bk, Wv, bv, Wp, bp):
        import jax, jax.numpy as jnp
        import numpy as np
        N_EMBD = 128
        COND = 128
        N_HEAD = 16
        B, N, NTOK = (4, 256, 256)
        Bx, Nx, C = x.shape
        H = N_HEAD
        D = C // H
        q = (x @ Wq.T + bq).reshape(Bx, Nx, H, D)
        k = (encoder_output @ Wk.T + bk).reshape(Bx, -1, H, D)
        v = (encoder_output @ Wv.T + bv).reshape(Bx, -1, H, D)
        scale = 1.0 / jnp.sqrt(jnp.asarray(D, x.dtype))
        att = jnp.einsum('bnhd,bthd->bhnt', q, k) * scale
        att = jax.nn.softmax(att, axis=-1)
        y = jnp.einsum('bhnt,bthd->bnhd', att, v).reshape(Bx, Nx, C)
        y = y @ Wp.T + bp
        return y

    def _L1_ffn_ref(inputs, Wr, br, W1, b1, W2, b2):
        import jax, jax.numpy as jnp
        import numpy as np
        B, T, D = inputs.shape
        E = Wr.shape[1]
        x = inputs.reshape(B * T, D)
        N = x.shape[0]
        C = N // E
        logits = x @ Wr + br
        probs = jax.nn.softmax(logits, axis=-1)
        gate = jnp.max(probs, axis=-1, keepdims=True)
        idx = jnp.argmax(probs, axis=-1)
        mask = jax.nn.one_hot(idx, E, dtype=jnp.float32)
        pos = (jnp.cumsum(mask, axis=0) * mask).astype(jnp.int32)
        mask = mask * (pos < C).astype(jnp.float32)
        mask_flat = jnp.sum(mask, axis=-1, keepdims=True)
        gate = gate * mask_flat
        combine = (gate * mask_flat * jax.nn.one_hot(idx, E, dtype=jnp.float32))[..., None] * jax.nn.one_hot(pos, C, dtype=jnp.float32)
        dispatch = combine
        expert_in = jnp.einsum('nd,nec->ecd', x, dispatch)
        h = jax.nn.relu(jnp.einsum('ecd,edf->ecf', expert_in, W1) + b1[:, None, :])
        eo = jnp.einsum('ecf,efd->ecd', h, W2) + b2[:, None, :]
        out = jnp.einsum('ecd,nec->nd', eo, combine)
        return out.reshape(B, T, D)
    x = x + jnp.tanh(g_xattn[0]) * _L0_xattn_ref(ctx_1024, ctx_1024, _layernorm(x, axis=-1), L0_xattn_Wk, L0_xattn_Wv, L0_xattn_bv, L0_xattn_Wq, L0_xattn_bq, L0_xattn_Wo, L0_xattn_bo)
    x = x + jnp.tanh(g_ffn[0]) * _L0_ffn_ref(_layernorm(x, axis=-1), L0_ffn_We, L0_ffn_be, L0_ffn_Wg, L0_ffn_bg)
    x = x + jnp.tanh(g_xattn[1]) * _L1_xattn_ref(_layernorm(x, axis=-1), ctx_1024, L1_xattn_Wq, L1_xattn_bq, L1_xattn_Wk, L1_xattn_bk, L1_xattn_Wv, L1_xattn_bv, L1_xattn_Wp, L1_xattn_bp)
    x = x + jnp.tanh(g_ffn[1]) * _L1_ffn_ref(_layernorm(x, axis=-1), L1_ffn_Wr, L1_ffn_br, L1_ffn_W1, L1_ffn_b1, L1_ffn_W2, L1_ffn_b2)
    return x

_drawn_inputs = setup_inputs


def setup_inputs(seed=0):
    import zlib

    import numpy as np

    out = dict(_drawn_inputs(seed))
    spreads = {'g_ffn': (-1.0, 0.6),
     'L0_xattn_bv': (0.0, 0.1),
     'L0_xattn_bq': (0.0, 0.1),
     'L0_xattn_bo': (0.0, 0.1),
     'L1_xattn_bq': (0.0, 0.8),
     'L1_xattn_bk': (0.0, 0.8),
     'L1_xattn_bv': (0.0, 0.431),
     'L1_xattn_bp': (0.0, 0.1),
     'L1_ffn_br': (0.0, 0.8),
     'L1_ffn_b1': (0.0, 0.8),
     'L1_ffn_b2': (0.0, 0.687)}
    factors = {'L1_xattn_Wq': 8.0,
     'L1_xattn_Wk': 8.0,
     'L1_ffn_Wr': 5.307,
     'L1_ffn_W1': 8.0,
     'L1_ffn_W2': 8.0}
    for name, (base, spread) in spreads.items():
        noise = np.random.default_rng([zlib.crc32(name.encode()), seed]).standard_normal(out[name].shape)
        drawn = base * np.exp(spread * noise) if base else spread * noise
        out[name] = jnp.asarray(drawn.astype(out[name].dtype))
    for name, factor in factors.items():
        out[name] = (out[name] * factor).astype(out[name].dtype)
    return out
```

```python
from contextlib import ExitStack

import concourse.bass as bass
from concourse import mybir

F32 = mybir.dt.float32
BF16 = mybir.dt.bfloat16
U32 = mybir.dt.uint32
ALU = mybir.AluOpType
ACT = mybir.ActivationFunctionType
AX_X = mybir.AxisListType.X

P = 128
D = 128
SEQ = 64
TG = 2
NB = TG * P // SEQ
E = 8
H = 16
DH = D // H
NJ = H // 2
EPS = 1e-5
SCALE0 = float(D) ** -0.5
SCALE1 = float(DH) ** -0.5
NU = E // 2
ORDER = {
    "tensor": """
a0 f0 m1 m2 a1 f1 m3 a2 f2 f3 a3 m4 f4 m5 f5 a4 a5 a6 a7 m6 f6 m7 f7 a8 m8 f8 a9 m9 a10 m10 f9 a11 f10 m11
m12 a12 f11 f12 m13
""".split(),
    "vector": """
m0 a0 f0 m2 m3 f2 f3 a3 f4 a4 f5 a6 a7 f7 a8 a9 f8 m9 f9 m10 f10 a11 f11 m11 m12 a12 f12 m13 f13
""".split(),
    "scalar": """
f0 m1 a1 f1 a2 m2 f2 m3 f3 m4 f4 a3 a4 a5 m5 f6 m6 a6 m7 m8 f7 a9 a10 f10
""".split(),
    "gpsimd": """
m0 a0 f0 m1 a2 k1 k2 f5 k3 k4
""".split(),
}


NORM = {"_stats": TG, "_mv": TG, "_eps": 1, "_rstd": 1, "_mneg": 1, "_nmr": 1, "_xn": TG}
PER_GROUP = {
    "x_loaded": 16, "ctx_loaded": 16, "out_stored": 16,
    **{n + k: c for n in ("n1", "n2", "n3", "n4") for k, c in NORM.items()},
    "f_ctxT_ps": 1, "f_ctxT": 1, "f_xnT_ps": 1, "f_xnT": 1, "f_q_ps": 1, "f_q": 1, "f_v_ps": 1, "f_v": 1,
    "f_s_ps": 1, "f_max": 2, "f_negmax": 1, "f_p": 2 * TG, "f_rinv": 1, "f_pT_ps": 1, "f_pT": 1,
    "f_pv_ps": 1, "f_x1": TG, "f_xn2T_ps": 1, "f_xn2T": 1,
    "f_r_ps": 1, "f_lg": 1, "f_neg": 1, "f_top": TG, "f_idx": TG, "f_idxf": 1, "f_oh1": TG, "f_oh": TG,
    "f_ex": TG, "f_sel": TG, "f_rsum": 1, "f_w": TG, "f_e_ps": NU, "f_chain": NU * 4, "f_wT_ps": 1, "f_wT": 1,
    "f_b_ps": 1, "f_out": 1,
    "a_k_ps": 1, "a_k": 1, "a_v_ps": 1, "a_v": TG, "a_kx": NB, "a_xb": 1, "a_xnT_ps": 1, "a_xnT": 1,
    "a_q_ps": 1, "a_q": 1, "a_s_ps": 2 * TG, "a_max": 2 * TG, "a_sub": 2 * TG, "a_p": 2 * TG, "a_sum": 2 * TG, "a_rinv": TG,
    "a_rE": 2 * TG, "a_pT_ps": 2 * TG, "a_pT": 2 * TG, "a_rT_ps": TG, "a_rT": TG, "a_y_ps": TG, "a_y": TG,
    "a_o_ps": TG, "a_x2": TG,
    "m_x2": 1, "m_xnT_ps": 1, "m_xnT": 1, "m_r_ps": 1, "m_lg": 1, "m_neg": 1, "m_top": TG, "m_idx": TG,
    "m_idxf": 1, "m_se": TG, "m_oh": TG, "m_c_ps": 1, "m_kw": 1, "m_gate": 1, "m_w": TG, "m_macc": 2,
    "m_xg": TG, "m_xgT_ps": 1, "m_xgT": 1, "m_wT_ps": 1, "m_wT": 1, "m_h_ps": NU, "m_h": E, "m_e_ps": NU,
    "m_chain": NU * 4, "m_b_ps": 1, "m_out": 1,
}
SETUP = ["w_attn0", "w_exp0", "w_attn1", "w_exp1", "w_rows", "w_cols", "i_zero", "i_ident", "i_one", "i_sel",
         "i_iota", "i_dve", "i_conv", "i_tanh", "i_ps", "i_ev", "i_wps", "i_wev", "i_bias"]


def build_program(nc, a, out):
    n_tok = a["x"].shape[0] * a["x"].shape[1]
    NG = n_tok // (TG * P)
    CAP = n_tok // E
    x_v = a["x"].rearrange("b s d -> (b s) d").rearrange("(g t p) d -> g p t d", t=TG, p=P)
    c_v = a["ctx_1024"].rearrange("b s d -> (b s) d").rearrange("(g t p) d -> g p t d", t=TG, p=P)
    o_v = out.rearrange("b s d -> (b s) d").rearrange("(g t p) d -> g p t d", t=TG, p=P)

    with ExitStack() as ctx:
        def sb(name, shape, dt=F32):
            return ctx.enter_context(nc.sbuf_tensor(name, shape, dt))

        def psum(name, shape, dt=F32):
            return ctx.enter_context(nc.psum_tensor(name, shape, dt))

        S = {n: ctx.enter_context(nc.semaphore(n)) for n in list(PER_GROUP) + SETUP}

        def after(eng, name, g, n):
            eng.wait_ge(S[name], g * PER_GROUP[name] + n)

        zero = sb("zero", [P, P])
        ident = sb("ident", [P, P])
        ones = sb("ones", [P, P])
        tri_f = sb("tri_f", [P, P])
        tri = sb("tri", [P, P], BF16)
        ones_bf = sb("ones_bf", [P, P], BF16)
        head_mask = sb("head_mask", [P, H])
        pair_mask = sb("pair_mask", [P, 2, DH])
        seq_mask = sb("seq_mask", [P, 2])
        iota_u = sb("iota_u", [P, E], U32)
        iota = sb("iota", [P, E])
        half_neg = sb("half_neg", [P, TG])
        eps = sb("eps", [P, TG])
        minus = sb("minus", [P, TG])
        w0 = sb("w0", [P, 4, D])
        w1 = sb("w1", [P, 4, D])
        w_e0 = sb("w_e0", [P, E + E * D])
        w_r1 = sb("w_r1", [P, E])
        w_up = sb("w_up", [P, E, D])
        w_dn = sb("w_dn", [P, E, D])
        be0 = sb("be0", [E, D])
        be1 = sb("be1", [E, D])
        b_up_rows = sb("b_up_rows", [E, D])
        cols = sb("cols", [P, 5])
        bo_bc = sb("bo_bc", [P, D])
        bp_bc = sb("bp_bc", [P, D])
        rb_bc = sb("rb_bc", [P, 2, E])
        g_bc = sb("g_bc", [P, 4])
        tg = sb("tg", [P, 4])
        wqk = sb("wqk", [P, D])
        bqk = sb("bqk", [P, 1])
        woT = sb("woT", [P, D])
        wvo = sb("wvo", [P, D])
        bv_bc = sb("bv_bc", [P, 2, P])
        vo_bias = sb("vo_bias", [P, D])
        w1T = sb("w1T", [P, 4, D])
        wp_dup = sb("wp_dup", [P, 2, 4, 2, 2 * DH])
        wpE = sb("wpE", [P, 2, D])
        p_bias = sb("p_bias", [P, D])
        b_upT = sb("b_upT", [P, E])
        x_in = sb("x_in", [P, TG, D])
        ctx_in = sb("ctx_in", [P, TG, D])
        wait_carrier = sb("wait_carrier", [P, 1])
        stats = {n: sb(n + "_st", [P, TG, 6]) for n in ("n1", "n2", "n3", "n4")}
        mv = {n: sb(n + "_mvb", [P, TG, 2]) for n in stats}
        ve = {n: sb(n + "_ve", [P, TG]) for n in stats}
        mneg = {n: sb(n + "_mnegb", [P, TG]) for n in stats}
        nmr = {n: sb(n + "_nmrb", [P, TG]) for n in stats}
        rstd = {n: sb(n + "_rs", [P, TG]) for n in stats}
        xn = {n: sb(n + "_xnb", [P, TG, D]) for n in stats}
        ctxT = sb("ctxT", [P, TG * P])
        xnT = sb("xnT", [P, TG * P])
        qT = sb("qT", [P, TG * P])
        vo = sb("vo", [P, TG, D])
        mx0 = sb("mx0", [P, TG])
        nmx0 = sb("nmx0", [P, TG])
        p0 = sb("p0", [P, TG, P])
        rs0 = sb("rs0", [P, TG])
        ri0 = sb("ri0", [P, TG])
        p0T = sb("p0T", [P, TG, P])
        x1 = sb("x1", [P, TG, D])
        xn2T = sb("xn2T", [P, TG * P])
        lg0 = sb("lg0", [P, TG, E])
        top0 = sb("top0", [P, TG, 8])
        idx0 = sb("idx0", [P, TG, 8], U32)
        idx0f = sb("idx0f", [P, TG, 2])
        neg0 = sb("neg0", [P, TG])
        ex0 = sb("ex0", [P, TG, E])
        oh0a = sb("oh0a", [P, TG, E])
        oh0 = sb("oh0", [P, TG, E])
        sel0 = sb("sel0", [P, TG, E])
        sum0 = sb("sum0", [P, TG])
        rsum0 = sb("rsum0", [P, TG])
        w_tok0 = sb("w_tok0", [P, TG, E])
        wT0 = sb("wT0", [E, TG * P])
        acc0 = sb("acc0", [P, TG, D])
        x_mid = sb("x_mid", [P, TG, D])
        k1T = sb("k1T", [P, NB, SEQ])
        kx = sb("kx", [P, NB, H, SEQ])
        vx = sb("vx", [P, TG, NJ, 2, 2 * DH])
        xb = sb("xb", [P, TG, D])
        xn3T = sb("xn3T", [P, TG * P])
        q1T = sb("q1T", [P, TG * P])
        mx1 = sb("mx1", [P, H])
        p1 = sb("p1", [P, H, SEQ])
        rs1 = sb("rs1", [P, H])
        ri1 = sb("ri1", [P, H])
        rE = sb("rE", [P, NJ, 2, 2, DH])
        p1T = sb("p1T", [P, NJ, P])
        rT = sb("rT", [P, 2, P])
        yT = sb("yT", [P, 2, P])
        x2 = sb("x2", [P, TG, D])
        xn4T = sb("xn4T", [P, TG * P])
        lg1 = sb("lg1", [P, TG, E])
        top1 = sb("top1", [P, TG, 8])
        idx1 = sb("idx1", [P, TG, 8], U32)
        idx1f = sb("idx1f", [P, TG, 1])
        neg1 = sb("neg1", [P, TG])
        ex1 = sb("ex1", [P, TG, E])
        se1 = sb("se1", [P, TG])
        gate1 = sb("gate1", [P, TG])
        oh1 = sb("oh1", [P, TG, E], BF16)
        macc = sb("macc", [P, E], BF16)
        kw1 = sb("kw1", [P, TG, E])
        w_tok1 = sb("w_tok1", [P, TG, E])
        xg = sb("xg", [P, TG, D])
        xgT = sb("xgT", [P, TG * P])
        wT1 = sb("wT1", [E, TG * P])
        hT = sb("hT", [P, E, TG * P])
        o_sb = sb("o_sb", [P, TG, D])
        fa = psum("fa", [P, 512])
        fe = psum("fe", [P, 2, 512])
        bs = psum("bs", [P, 2, 512])
        bm = psum("bm", [P, 512])
        bc = psum("bc", [P, 2, 512])

        def run(eng, order, front, attn, moe, keys=None):
            def steps(i, has_f, has_a, has_m):
                for step in order:
                    s = int(step[1:])
                    if step[0] == "f" and has_f:
                        front(i, s)
                    if step[0] == "k" and has_f and keys is not None:
                        keys(i, s)
                    if step[0] == "a" and has_a:
                        attn(i - 1, s)
                    if step[0] == "m" and has_m:
                        moe(i - 2, s)

            steps(0, True, False, False)
            steps(1, True, True, False)
            steps(2, True, True, True)
            with eng.Fori(3, NG) as i:
                steps(i, True, True, True)
            steps(NG, False, True, True)
            steps(NG + 1, False, False, True)

        def later(g):
            return not (isinstance(g, int) and g == 0)

        block = ctx.enter_context(nc.Block())

        @block.sync
        def _(sp):
            def load(g):
                if later(g):
                    after(sp, "f_x1", g - 1, TG)
                sp.dma_start(x_in[:, :, :], x_v[g]).then_inc(S["x_loaded"], 16)
                sp.dma_start(ctx_in[:, :, :], c_v[g]).then_inc(S["ctx_loaded"], 16)

            def store(g):
                after(sp, "m_out", g, 1)
                sp.dma_start(o_v[g], o_sb[:, :, :]).then_inc(S["out_stored"], 16)

            load(0)
            for n, name in enumerate(("Wq", "Wk", "Wv", "Wo")):
                sp.dma_start(w0[:, n, :], a["L0_xattn_" + name]).then_inc(S["w_attn0"], 16)
            sp.dma_start(w_e0[:, 0:E], a["L0_ffn_Wg"]).then_inc(S["w_exp0"], 16)
            sp.dma_start(w_e0[:, E:].rearrange("p (e o) -> p e o", e=E),
                         a["L0_ffn_We"].rearrange("e d o -> d e o")).then_inc(S["w_exp0"], 16)
            sp.dma_start(be0[:, :], a["L0_ffn_be"]).then_inc(S["w_exp0"], 16)
            load(1)
            sp.dma_start(w_r1[:, :], a["L1_ffn_Wr"]).then_inc(S["w_exp1"], 16)
            sp.dma_start(w_up[:, :, :], a["L1_ffn_W1"].rearrange("e d f -> d e f")).then_inc(S["w_exp1"], 16)
            sp.dma_start(w_dn[:, :, :], a["L1_ffn_W2"].rearrange("e f d -> f e d")).then_inc(S["w_exp1"], 16)
            sp.dma_start(be1[:, :], a["L1_ffn_b2"]).then_inc(S["w_exp1"], 16)
            load(2)
            load(3)
            with sp.Fori(0, NG - 4) as g:
                store(g)
                load(g + 4)
            for g in range(NG - 4, NG):
                store(g)
            sp.wait_ge(S["out_stored"], 16 * NG)

        @block.scalar
        def _(act):
            for n, src in enumerate((a["g_xattn"], a["g_ffn"])):
                act.dma_start(g_bc[:, 2 * n:2 * n + 2], src.partition_broadcast(P)).then_inc(S["w_rows"], 16)
            for n, name in enumerate(("L0_xattn_bq", "L0_xattn_bv", "L1_xattn_bq", "L1_xattn_bk", "L1_xattn_bv")):
                act.dma_start(cols[:, n:n + 1], a[name].rearrange("(p o) -> p o", o=1)).then_inc(S["w_cols"], 16)
            act.dma_start(bo_bc[:, :], a["L0_xattn_bo"].partition_broadcast(P)).then_inc(S["w_rows"], 16)
            for n, name in enumerate(("L0_ffn_bg", "L1_ffn_br")):
                act.dma_start(rb_bc[:, n, :], a[name].partition_broadcast(P)).then_inc(S["w_rows"], 16)
            act.dma_start(bp_bc[:, :], a["L1_xattn_bp"].partition_broadcast(P)).then_inc(S["w_rows"], 16)
            act.dma_start(b_up_rows[:, :], a["L1_ffn_b1"]).then_inc(S["w_rows"], 16)
            for n, name in enumerate(("Wq", "Wk", "Wv", "Wp")):
                act.dma_start(w1[:, n, :], a["L1_xattn_" + name]).then_inc(S["w_attn1"], 16)
            act.wait_ge(S["w_rows"], 16 * 7)
            nc.scalar.activation(tg[:, :], g_bc[:, :], ACT.Tanh).then_inc(S["i_tanh"], 1)

            def copy(dst, src, name, bias=None):
                if bias is None:
                    return nc.scalar.copy(dst, src).then_inc(S[name], 1)
                return nc.scalar.activation(dst, src, ACT.Identity, bias=bias).then_inc(S[name], 1)

            def norm_apply(n, src, g):
                after(act, n + "_nmr", g, 1)
                for t in range(TG):
                    nc.scalar.activation(xn[n][:, t, :], src[:, t, :], ACT.Identity, bias=nmr[n][:, t:t + 1],
                                         scale=rstd[n][:, t:t + 1]).then_inc(S[n + "_xn"], 1)

            def front(g, s):
                if s == 0:
                    if later(g):
                        after(act, "a_v_ps", g - 1, 1)
                    after(act, "f_ctxT_ps", g, 1)
                    copy(ctxT[:, :], fa[:, 0:TG * P], "f_ctxT")
                if s == 1:
                    norm_apply("n1", x_in, g)
                    after(act, "f_xnT_ps", g, 1)
                    copy(xnT[:, :], fe[:, 0, 0:TG * P], "f_xnT")
                    if later(g):
                        after(act, "a_kx", g - 1, NB)
                    after(act, "a_k_ps", g, 1)
                    copy(k1T[:, :, :], fa[:, 0:TG * P].rearrange("p (b k) -> p b k", b=NB), "a_k", bias=cols[:, 3:4])
                if s == 2:
                    after(act, "f_q_ps", g, 1)
                    copy(qT[:, :], fa[:, 0:TG * P], "f_q", bias=bqk[:, 0:1])
                if s == 3:
                    after(act, "f_negmax", g, 1)
                    for t in range(TG):
                        for b in range(2):
                            r = slice(SEQ * b, SEQ * b + SEQ)
                            nc.scalar.activation(p0[r, t, r], fa[r, t * P + SEQ * b:t * P + SEQ * b + SEQ], ACT.Exp,
                                                 bias=nmx0[r, t:t + 1], scale=SCALE0,
                                                 accum_out=rs0[r, t:t + 1]).then_inc(S["f_p"], 1)
                if s == 4:
                    after(act, "f_pT_ps", g, 1)
                    copy(p0T[:, :, :], fe[:, 0, 0:TG * P].rearrange("p (t q) -> p t q", t=TG), "f_pT")
                if s == 6:
                    norm_apply("n2", x1, g)
                    after(act, "f_xn2T_ps", g, 1)
                    copy(xn2T[:, :], fe[:, 0, 0:TG * P], "f_xn2T")
                if s == 7:
                    after(act, "f_neg", g, 1)
                    for t in range(TG):
                        nc.scalar.activation(ex0[:, t, :], lg0[:, t, :], ACT.Exp,
                                             bias=neg0[:, t:t + 1]).then_inc(S["f_ex"], 1)
                if s == 10:
                    after(act, "f_wT_ps", g, 1)
                    copy(wT0[:, :], fa[0:E, 0:TG * P], "f_wT")

            def attn(g, s):
                if s == 1:
                    norm_apply("n3", x_mid, g)
                    after(act, "a_xnT_ps", g, 1)
                    copy(xn3T[:, :], bm[:, 0:TG * P], "a_xnT")
                if s == 2:
                    after(act, "a_q_ps", g, 1)
                    copy(q1T[:, :], bm[:, 0:TG * P], "a_q", bias=cols[:, 2:3])
                if s in (3, 6):
                    t = s // 6
                    for c in range(2):
                        hs = slice(c * H // 2, (c + 1) * H // 2)
                        after(act, "a_sub", g, 2 * t + c + 1)
                        nc.scalar.activation(p1[:, hs, :], p1[:, hs, :], ACT.Exp, scale=SCALE1).then_inc(S["a_p"], 1)
                if s in (4, 9):
                    t = s // 9
                    for c in range(2):
                        after(act, "a_pT_ps", g, 2 * t + c + 1)
                        copy(p1T[:, 4 * c:4 * c + 4, :], bs[:, c, :].rearrange("p (j q) -> p j q", j=4), "a_pT")
                if s in (5, 10):
                    t = s // 10
                    after(act, "a_rT_ps", g, t + 1)
                    copy(rT[:, :, :], bm[:, 0:2 * P].rearrange("p (m q) -> p m q", m=2), "a_rT")

            def moe(g, s):
                if s == 1:
                    norm_apply("n4", x2, g)
                    after(act, "m_xnT_ps", g, 1)
                    copy(xn4T[:, :], bc[:, 0, 0:TG * P], "m_xnT")
                if s == 2:
                    after(act, "m_neg", g, 1)
                    for t in range(TG):
                        nc.scalar.activation(ex1[:, t, :], lg1[:, t, :], ACT.Exp, bias=neg1[:, t:t + 1],
                                             accum_out=se1[:, t:t + 1]).then_inc(S["m_se"], 1)
                if s == 3:
                    after(act, "m_gate", g, 1)
                    for t in range(TG):
                        nc.scalar.activation(xg[:, t, :], xn["n4"][:, t, :], ACT.Copy,
                                             scale=gate1[:, t:t + 1]).then_inc(S["m_xg"], 1)
                if s == 4:
                    after(act, "m_xgT_ps", g, 1)
                    copy(xgT[:, :], bc[:, 1, 0:TG * P], "m_xgT")
                    after(act, "m_wT_ps", g, 1)
                    copy(wT1[:, :], bc[0:E, 0, 0:TG * P], "m_wT")
                if 5 <= s < 5 + NU:
                    u = s - 5
                    if u == 0 and later(g):
                        after(act, "m_e_ps", g - 1, NU)
                    after(act, "m_h_ps", g, u + 1)
                    for e in (2 * u, 2 * u + 1):
                        nc.scalar.activation(hT[:, e, :], bc[:, u % 2, TG * P * (e % 2):TG * P * (e % 2 + 1)], ACT.Relu,
                                             bias=b_upT[:, e:e + 1]).then_inc(S["m_h"], 1)

            run(act, ORDER["scalar"], front, attn, moe)

        @block.gpsimd
        def _(pool):
            nc.gpsimd.memset(zero[:, :], 0.0).then_inc(S["i_zero"], 1)
            nc.gpsimd.memset(ones[:, :], 1.0).then_inc(S["i_one"], 1)
            nc.gpsimd.iota(iota_u[:, :], pattern=[[1, E]], base=0, channel_multiplier=0).then_inc(S["i_iota"], 1)
            nc.gpsimd.memset(half_neg[:, :], -0.5).then_inc(S["i_one"], 1)
            nc.gpsimd.memset(eps[:, :], EPS).then_inc(S["i_one"], 1)
            nc.gpsimd.memset(minus[:, :], -1.0).then_inc(S["i_one"], 1)
            pool.wait_ge(S["i_zero"], 1)
            nc.gpsimd.affine_select(out=ident[:, :], in_=zero[:, :], compare_op=ALU.not_equal, fill=1.0, base=0,
                                    pattern=[[-1, P]], channel_multiplier=1).then_inc(S["i_ident"], 1)
            pool.wait_ge(S["i_one"], 4)
            nc.gpsimd.affine_select(out=tri_f[:, :], in_=ones[:, :], compare_op=ALU.is_ge, fill=0.0, base=0,
                                    pattern=[[1, P]], channel_multiplier=-1).then_inc(S["i_sel"], 1)
            nc.gpsimd.affine_select(out=head_mask[:, :], in_=ones[:, 0:H], compare_op=ALU.is_ge, fill=0.0, base=0,
                                    pattern=[[-DH, H]], channel_multiplier=1).then_inc(S["i_sel"], 1)
            pool.wait_ge(S["i_sel"], 2)
            nc.gpsimd.affine_select(out=head_mask[:, :], in_=head_mask[:, :], compare_op=ALU.is_ge, fill=0.0,
                                    base=DH - 1, pattern=[[DH, H]], channel_multiplier=-1).then_inc(S["i_sel"], 1)
            pool.wait_ge(S["i_sel"], 3)

            def rstd_of(n, g):
                tt = nc.gpsimd.tensor_tensor
                after(pool, n + "_mv", g, TG)
                tt(ve[n][:, :], mv[n][:, :, 1], eps[:, :], ALU.add).then_inc(S[n + "_eps"], 1)
                tt(mneg[n][:, :], mv[n][:, :, 0], minus[:, :], ALU.mult).then_inc(S[n + "_mneg"], 1)
                after(pool, n + "_eps", g, 1)
                tt(rstd[n][:, :], ve[n][:, :], half_neg[:, :], ALU.pow).then_inc(S[n + "_rstd"], 1)
                after(pool, n + "_mneg", g, 1)
                after(pool, n + "_rstd", g, 1)
                tt(nmr[n][:, :], mneg[n][:, :], rstd[n][:, :], ALU.mult).then_inc(S[n + "_nmr"], 1)

            def spread_keys(g, b):
                nc.gpsimd.tensor_tensor(kx[:, b, :, :], k1T[:, b, :].unsqueeze(1).to_broadcast([P, H, SEQ]),
                                        head_mask[:, :].unsqueeze(2).to_broadcast([P, H, SEQ]),
                                        ALU.mult).then_inc(S["a_kx"], 1)

            def front(g, s):
                if s == 0:
                    rstd_of("n1", g)
                if s == 5:
                    rstd_of("n2", g)

            def attn(g, s):
                if s == 0:
                    rstd_of("n3", g)
                if s == 2:
                    if later(g):
                        after(pool, "a_x2", g - 1, TG)
                    if isinstance(g, int) and g == 0:
                        pool.wait_ge(S["i_bias"], 2)
                    after(pool, "f_out", g, 1)
                    nc.gpsimd.tensor_tensor(xb[:, :, :], x_mid[:, :, :],
                                            p_bias[:, :].unsqueeze(1).to_broadcast([P, TG, D]),
                                            ALU.add).then_inc(S["a_xb"], 1)

            def keys(g, s):
                if s in (1, 3):
                    if later(g):
                        after(pool, "a_s_ps", g - 1, s + 1)
                    after(pool, "a_k", g, 1)
                spread_keys(g, s - 1)

            def moe(g, s):
                if s == 0:
                    rstd_of("n4", g)
                if s == 1:
                    if later(g):
                        after(pool, "out_stored", g - 1, 16)
                    after(pool, "a_x2", g, TG)
                    nc.gpsimd.tensor_tensor(o_sb[:, :, :], x2[:, :, :], zero[:, :].unsqueeze(1).to_broadcast([P, TG, D]),
                                            ALU.add).then_inc(S["m_x2"], 1)

            run(pool, ORDER["gpsimd"], front, attn, moe, keys)

        @block.vector
        def _(dve):
            V = nc.vector
            V.memset(pair_mask[:, :, :], 0.0).then_inc(S["i_dve"], 1)
            V.memset(seq_mask[:, :], 0.0).then_inc(S["i_dve"], 1)
            V.memset(p0[:, :, :], 0.0).then_inc(S["i_dve"], 1)
            V.memset(macc[:, :], 0.0).then_inc(S["i_dve"], 1)
            dve.wait_ge(S["i_dve"], 4)
            for b in range(2):
                r = slice(SEQ * b, SEQ * b + SEQ)
                V.memset(pair_mask[r, b, :], 1.0).then_inc(S["i_dve"], 1)
                V.memset(seq_mask[r, b:b + 1], 1.0).then_inc(S["i_dve"], 1)
            dve.wait_ge(S["i_iota"], 1)
            V.tensor_copy(iota[:, :], iota_u[:, :]).then_inc(S["i_conv"], 1)
            dve.wait_ge(S["i_sel"], 3)
            V.tensor_copy(tri[:, :], tri_f[:, :]).then_inc(S["i_conv"], 1)
            V.tensor_copy(ones_bf[:, :], ones[:, :]).then_inc(S["i_conv"], 1)
            dve.wait_ge(S["w_cols"], 16 * 5)
            V.tensor_scalar(bv_bc[:, 0, :], ones[:, :], cols[:, 1:2], None, ALU.mult).then_inc(S["i_conv"], 1)
            V.tensor_scalar(bv_bc[:, 1, :], ones[:, :], cols[:, 4:5], None, ALU.mult).then_inc(S["i_conv"], 1)
            dve.wait_ge(S["w_attn1"], 16 * 4)
            for b in range(2):
                V.tensor_copy(wp_dup[:, :, :, b, :],
                              w1[:, 3, :].rearrange("p (m j c) -> p m j c", m=2, j=4)).then_inc(S["i_conv"], 1)
            dve.wait_ge(S["i_tanh"], 1)
            dve.wait_ge(S["i_ps"], 1)
            V.tensor_copy(woT[:, :], fa[:, 0:D]).then_inc(S["i_ev"], 1)
            V.tensor_copy(wqk[:, :], fa[:, D:2 * D]).then_inc(S["i_ev"], 1)
            V.tensor_copy(bqk[:, :], fa[:, 2 * D:2 * D + 1]).then_inc(S["i_ev"], 1)
            dve.wait_ge(S["i_ps"], 2)
            V.tensor_scalar(wvo[:, :], bc[:, 0, 0:D], tg[:, 0:1], None, ALU.mult).then_inc(S["i_ev"], 1)
            V.tensor_tensor(vo_bias[:, :], bc[:, 0, D:2 * D], bo_bc[:, :], ALU.add).then_inc(S["i_bias"], 1)
            dve.wait_ge(S["i_bias"], 1)
            V.tensor_scalar(vo_bias[:, :], vo_bias[:, :], tg[:, 0:1], None, ALU.mult).then_inc(S["i_ev"], 1)
            dve.wait_ge(S["i_ev"], 5)

            dve.wait_ge(S["i_wps"], 1)
            V.tensor_copy(w1T[:, :, :], bs[:, 0, :].rearrange("p (n d) -> p n d", n=4)).then_inc(S["i_wev"], 1)

            def finish_block1():
                dve.wait_ge(S["i_wps"], 2)
                V.tensor_scalar(wpE[:, :, :], bm[:, 0:2 * D].rearrange("p (m d) -> p m d", m=2), tg[:, 1:2], None,
                                ALU.mult).then_inc(S["i_wev"], 1)
                V.tensor_copy(b_upT[:, :], bm[:, 2 * D:2 * D + E]).then_inc(S["i_wev"], 1)
                dve.wait_ge(S["i_wps"], 3)
                V.tensor_tensor(p_bias[:, :], bs[:, 1, 0:D], bp_bc[:, :], ALU.add).then_inc(S["i_wev"], 1)
                dve.wait_ge(S["i_wev"], 4)
                V.tensor_scalar(p_bias[:, :], p_bias[:, :], tg[:, 1:2], None, ALU.mult).then_inc(S["i_bias"], 1)

            def norm(n, src, g):
                for t in range(TG):
                    V.bn_stats(stats[n][:, t, :], src[:, t, :]).then_inc(S[n + "_stats"], 1)
                after(dve, n + "_stats", g, TG)
                V.memset(wait_carrier[:, :], 0.0)
                for t in range(TG):
                    V.bn_aggr(mv[n][:, t, :], stats[n][:, t, :]).then_inc(S[n + "_mv"], 1)

            def combine(name, g, u, acc, first, w, bank):
                for n in range(4):
                    e, t = 2 * u + n // 2, n % 2
                    if u or n >= 2:
                        after(dve, name, g, 4 * u + n - 1)
                    V.scalar_tensor_tensor(out=acc[:, t, :], in0=bank[:, (2 * t + n // 2) * D:(2 * t + n // 2 + 1) * D],
                                           scalar=w[:, t, e:e + 1], in1=(acc if e else first)[:, t, :],
                                           op0=ALU.mult, op1=ALU.add).then_inc(S[name], 1)

            def logits(k, g, bank, row, lg, neg, top):
                after(dve, k + "_r_ps", g, 1)
                V.tensor_tensor(lg[:, :, :], bank[:, 0:TG * E].rearrange("p (t e) -> p t e", t=TG),
                                rb_bc[:, row:row + 1, :].to_broadcast([P, TG, E]), ALU.add).then_inc(S[k + "_lg"], 1)
                after(dve, k + "_lg", g, 1)
                V.tensor_reduce(neg[:, :], lg[:, :, :], AX_X, ALU.max, negate=True).then_inc(S[k + "_neg"], 1)
                for t in range(TG):
                    V.max(top[:, t, :], lg[:, t, :]).then_inc(S[k + "_top"], 1)

            def places(k, g, lg, top, idx, idxf, n):
                after(dve, k + "_top", g, TG)
                V.memset(wait_carrier[:, :], 0.0)
                for t in range(TG):
                    V.max_index(idx[:, t, :], top[:, t, :], lg[:, t, :]).then_inc(S[k + "_idx"], 1)
                after(dve, k + "_idx", g, TG)
                V.tensor_copy(idxf[:, :, :], idx[:, :, 0:n]).then_inc(S[k + "_idxf"], 1)
                after(dve, k + "_idxf", g, 1)

            def front(g, s):
                if s == 0:
                    after(dve, "x_loaded", g, 16)
                    norm("n1", x_in, g)
                if s == 2:
                    after(dve, "f_v_ps", g, 1)
                    V.tensor_tensor(vo[:, :, :], fe[:, 1, 0:TG * D].rearrange("p (t d) -> p t d", t=TG),
                                    vo_bias[:, :].unsqueeze(1).to_broadcast([P, TG, D]), ALU.add)\
                     .then_inc(S["f_v"], 1)
                if s == 3:
                    after(dve, "f_s_ps", g, 1)
                    for b in range(2):
                        r = slice(SEQ * b, SEQ * b + SEQ)
                        V.tensor_reduce(mx0[r, :], fa[r, 0:TG * P].rearrange("p (t k) -> p t k", t=TG)[:, :, r],
                                        AX_X, ALU.max).then_inc(S["f_max"], 1)
                    after(dve, "f_max", g, 2)
                    V.tensor_scalar(nmx0[:, :], mx0[:, :], -SCALE0, None, ALU.mult).then_inc(S["f_negmax"], 1)
                if s == 4:
                    after(dve, "f_p", g, 2 * TG)
                    V.reciprocal(ri0[:, :], rs0[:, :]).then_inc(S["f_rinv"], 1)
                if s == 5:
                    after(dve, "f_rinv", g, 1)
                    after(dve, "f_pv_ps", g, 1)
                    for t in range(TG):
                        V.scalar_tensor_tensor(out=x1[:, t, :], in0=fa[:, t * D:t * D + D], scalar=ri0[:, t:t + 1],
                                               in1=x_in[:, t, :], op0=ALU.mult, op1=ALU.add)\
                         .then_inc(S["f_x1"], 1)
                    after(dve, "f_x1", g, TG)
                    norm("n2", x1, g)
                if s == 7:
                    logits("f", g, fa, 0, lg0, neg0, top0)
                    places("f", g, lg0, top0, idx0, idx0f, 2)
                    for t in range(TG):
                        V.tensor_scalar(oh0a[:, t, :], iota[:, :], idx0f[:, t, 0:1], None, ALU.is_equal)\
                         .then_inc(S["f_oh1"], 1)
                    for t in range(TG):
                        after(dve, "f_oh1", g, t + 1)
                        V.scalar_tensor_tensor(out=oh0[:, t, :], in0=iota[:, :], scalar=idx0f[:, t, 1:2],
                                               in1=oh0a[:, t, :], op0=ALU.is_equal, op1=ALU.add)\
                         .then_inc(S["f_oh"], 1)
                if s == 8:
                    for t in range(TG):
                        after(dve, "f_oh", g, t + 1)
                        after(dve, "f_ex", g, t + 1)
                        V.tensor_tensor_reduce(sel0[:, t, :], ex0[:, t, :], oh0[:, t, :], 1.0, 0.0, ALU.mult, ALU.add,
                                               sum0[:, t:t + 1]).then_inc(S["f_sel"], 1)
                    after(dve, "f_sel", g, TG)
                    V.reciprocal(rsum0[:, :], sum0[:, :]).then_inc(S["f_rsum"], 1)
                    after(dve, "f_rsum", g, 1)
                    for t in range(TG):
                        V.tensor_scalar(w_tok0[:, t, :], sel0[:, t, :], rsum0[:, t:t + 1], tg[:, 2:3], ALU.mult,
                                        ALU.mult).then_inc(S["f_w"], 1)
                if 9 <= s < 9 + NU:
                    u = s - 9
                    if u == 0:
                        after(dve, "f_w", g, TG)
                    after(dve, "f_e_ps", g, u + 1)
                    combine("f_chain", g, u, acc0, x1, w_tok0, fe[:, u % 2, :])
                if s == 13:
                    after(dve, "f_chain", g, NU * 4)
                    if later(g):
                        after(dve, "a_xb", g - 1, 1)
                        after(dve, "n3_xn", g - 1, TG)
                    after(dve, "f_b_ps", g, 1)
                    V.tensor_tensor(x_mid[:, :, :], fa[:, 0:TG * D].rearrange("p (t d) -> p t d", t=TG),
                                    acc0[:, :, :], ALU.add).then_inc(S["f_out"], 1)

            def attn(g, s):
                if s == 0:
                    if isinstance(g, int) and g == 0:
                        finish_block1()
                    after(dve, "f_out", g, 1)
                    norm("n3", x_mid, g)
                    after(dve, "a_v_ps", g, 1)
                    for t in range(TG):
                        V.tensor_tensor(
                            vx[:, t, :, :, :],
                            bs[:, 0, t * 2 * D:(t + 1) * 2 * D].rearrange("p (b j c) -> p j b c", b=2, j=NJ),
                            pair_mask[:, :, :].rearrange("p h d -> p (h d)").unsqueeze(1).unsqueeze(1)
                            .to_broadcast([P, NJ, 2, 2 * DH]), ALU.mult).then_inc(S["a_v"], 1)
                if s in (3, 6):
                    t = s // 6
                    for c in range(2):
                        n, hs = 2 * t + c + 1, slice(c * H // 2, (c + 1) * H // 2)
                        sc = bs[:, c, :].rearrange("p (h k) -> p h k", h=H // 2)
                        after(dve, "a_s_ps", g, n)
                        V.tensor_reduce(mx1[:, hs], sc, AX_X, ALU.max).then_inc(S["a_max"], 1)
                        after(dve, "a_max", g, n)
                        V.tensor_tensor(p1[:, hs, :], sc, mx1[:, hs].unsqueeze(2).to_broadcast([P, H // 2, SEQ]),
                                        ALU.subtract).then_inc(S["a_sub"], 1)
                if s in (4, 9):
                    t = s // 9
                    for c in range(2):
                        hs = slice(c * H // 2, (c + 1) * H // 2)
                        after(dve, "a_p", g, 2 * t + c + 1)
                        V.tensor_reduce(rs1[:, hs], p1[:, hs, :], AX_X, ALU.add).then_inc(S["a_sum"], 1)
                    after(dve, "a_sum", g, 2 * t + 2)
                    V.reciprocal(ri1[:, :], rs1[:, :]).then_inc(S["a_rinv"], 1)
                    after(dve, "a_rinv", g, t + 1)
                    for b in range(2):
                        V.tensor_scalar(rE[:, :, b, :, :],
                                        ri1[:, :].rearrange("p (j h) -> p j h", h=2).unsqueeze(3)
                                        .to_broadcast([P, NJ, 2, DH]), seq_mask[:, b:b + 1], None,
                                        ALU.mult).then_inc(S["a_rE"], 1)
                if s in (7, 11):
                    t = s // 11
                    after(dve, "a_rT", g, t + 1)
                    after(dve, "a_y_ps", g, t + 1)
                    V.tensor_tensor(yT[:, :, :], bm[:, 0:2 * P].rearrange("p (m q) -> p m q", m=2), rT[:, :, :],
                                    ALU.mult).then_inc(S["a_y"], 1)
                if s in (8, 12):
                    t = s // 12
                    if t == 0:
                        after(dve, "a_xb", g, 1)
                        if later(g):
                            after(dve, "m_x2", g - 1, 1)
                            after(dve, "n4_xn", g - 1, TG)
                    after(dve, "a_o_ps", g, t + 1)
                    V.tensor_tensor(x2[:, t, :], bm[:, 0:D], xb[:, t, :], ALU.add).then_inc(S["a_x2"], 1)

            def moe(g, s):
                if s == 0:
                    after(dve, "a_x2", g, TG)
                    norm("n4", x2, g)
                if s == 2:
                    logits("m", g, bc[:, 1, :], 1, lg1, neg1, top1)
                    places("m", g, lg1, top1, idx1, idx1f, 1)
                    for t in range(TG):
                        V.tensor_scalar(oh1[:, t, :], iota[:, :], idx1f[:, t, :], None, ALU.is_equal)\
                         .then_inc(S["m_oh"], 1)
                    after(dve, "m_se", g, TG)
                    V.reciprocal(gate1[:, :], se1[:, :]).then_inc(S["m_gate"], 1)
                if s == 3:
                    after(dve, "m_oh", g, TG)
                    after(dve, "m_gate", g, 1)
                    after(dve, "m_c_ps", g, 1)
                    V.scalar_tensor_tensor(out=kw1[:, :, :], in0=bc[:, 0, 0:TG * E].rearrange("p (t e) -> p t e", t=TG),
                                           scalar=float(CAP), in1=oh1[:, :, :], op0=ALU.is_lt, op1=ALU.mult)\
                     .then_inc(S["m_kw"], 1)
                    V.tensor_tensor(macc[:, :], macc[:, :], oh1[:, 0, :], ALU.add).then_inc(S["m_macc"], 1)
                    after(dve, "m_kw", g, 1)
                    for t in range(TG):
                        V.tensor_scalar(w_tok1[:, t, :], kw1[:, t, :], gate1[:, t:t + 1], tg[:, 3:4], ALU.mult,
                                        ALU.mult).then_inc(S["m_w"], 1)
                    after(dve, "m_macc", g, 1)
                    V.tensor_tensor(macc[:, :], macc[:, :], oh1[:, 1, :], ALU.add).then_inc(S["m_macc"], 1)
                if 9 <= s < 9 + NU:
                    u = s - 9
                    if u == 0:
                        after(dve, "m_x2", g, 1)
                        after(dve, "m_w", g, TG)
                    after(dve, "m_e_ps", g, u + 1)
                    combine("m_chain", g, u, o_sb, o_sb, w_tok1, bc[:, u % 2, :])
                if s == 13:
                    after(dve, "m_chain", g, NU * 4)
                    after(dve, "m_b_ps", g, 1)
                    V.tensor_tensor(o_sb[:, :, :], bc[:, 0, 0:TG * D].rearrange("p (t d) -> p t d", t=TG),
                                    o_sb[:, :, :], ALU.add).then_inc(S["m_out"], 1)

            run(dve, ORDER["vector"], front, attn, moe)

        @block.tensor
        def _(pe):
            def mm(dst, lhsT, rhs, start=True, stop=True, **kw):
                return nc.tensor.matmul(dst, lhsT, rhs, start=start, stop=stop, **kw)

            def turn(dst, src):
                n = src.partition_size()
                return nc.tensor.transpose(dst, src, ident[0:n, 0:n])

            pe.wait_ge(S["i_ident"], 1)
            pe.wait_ge(S["w_attn0"], 16 * 4)
            pe.wait_ge(S["w_cols"], 16 * 5)
            turn(fa[:, 0:D], w0[:, 3, :])
            mm(fa[:, D:2 * D], w0[:, 0, :], w0[:, 1, :])
            mm(fa[:, 2 * D:2 * D + 1], w0[:, 1, :], cols[:, 0:1]).then_inc(S["i_ps"], 1)
            pe.wait_ge(S["i_ev"], 1)
            pe.wait_ge(S["i_conv"], 4)
            mm(bc[:, 0, 0:D], w0[:, 2, :], woT[:, :])
            mm(bc[:, 0, D:2 * D], bv_bc[:, 0, :], woT[:, :]).then_inc(S["i_ps"], 1)
            pe.wait_ge(S["w_attn1"], 16 * 4)
            for n in range(4):
                last = turn(bs[:, 0, n * D:n * D + D], w1[:, n, :])
            last.then_inc(S["i_wps"], 1)
            pe.wait_ge(S["i_conv"], 7)
            for m in range(2):
                turn(bm[:, m * D:m * D + D], wp_dup[:, m, :, :, :].rearrange("p j b c -> p (j b c)"))
            pe.wait_ge(S["w_rows"], 16 * 7)
            turn(bm[:, 2 * D:2 * D + E], b_up_rows[:, :]).then_inc(S["i_wps"], 1)
            pe.wait_ge(S["i_ev"], 5)

            def turn2(bank, src):
                for t in range(TG):
                    last = turn(bank[:, t * P:t * P + P], src[:, t, :])
                return last

            def front(g, s):
                if s == 0:
                    if later(g):
                        after(pe, "f_out", g - 1, 1)
                    after(pe, "ctx_loaded", g, 16)
                    turn2(fa, ctx_in).then_inc(S["f_ctxT_ps"], 1)
                if s == 1:
                    if isinstance(g, int) and g == 0:
                        pe.wait_ge(S["i_wev"], 1)
                    after(pe, "f_ctxT", g, 1)
                    mm(fa[:, 0:TG * P], w1T[:, 1, :], ctxT[:, :]).then_inc(S["a_k_ps"], 1)
                    after(pe, "n1_xn", g, TG)
                    turn2(fe[:, 0, :], xn["n1"]).then_inc(S["f_xnT_ps"], 1)
                if s == 2:
                    after(pe, "f_xnT", g, 1)
                    after(pe, "a_k", g, 1)
                    mm(fa[:, 0:TG * P], wqk[:, :], xnT[:, :]).then_inc(S["f_q_ps"], 1)
                    for t in range(TG):
                        last = mm(fe[:, 1, t * D:t * D + D], ctxT[:, t * P:t * P + P], wvo[:, :])
                    last.then_inc(S["f_v_ps"], 1)
                if s == 3:
                    after(pe, "f_q", g, 1)
                    for t in range(TG):
                        last = mm(fa[:, t * P:t * P + P], qT[:, t * P:t * P + P], ctxT[:, t * P:t * P + P])
                    last.then_inc(S["f_s_ps"], 1)
                if s == 4:
                    after(pe, "f_v", g, 1)
                    after(pe, "f_p", g, 2 * TG)
                    turn2(fe[:, 0, :], p0).then_inc(S["f_pT_ps"], 1)
                if s == 5:
                    after(pe, "f_pT", g, 1)
                    for t in range(TG):
                        last = mm(fa[:, t * D:t * D + D], p0T[:, t, :], vo[:, t, :])
                    last.then_inc(S["f_pv_ps"], 1)
                if s == 6:
                    after(pe, "n2_xn", g, TG)
                    turn2(fe[:, 0, :], xn["n2"]).then_inc(S["f_xn2T_ps"], 1)
                if s == 7:
                    after(pe, "f_xn2T", g, 1)
                    if isinstance(g, int) and g == 0:
                        pe.wait_ge(S["w_exp0"], 16 * 3)
                    for t in range(TG):
                        last = mm(fa[:, t * E:t * E + E], xn2T[:, t * P:t * P + P], w_e0[:, 0:E])
                    last.then_inc(S["f_r_ps"], 1)
                if 8 <= s < 8 + NU:
                    u = s - 8
                    if u >= 2:
                        after(pe, "f_chain", g, 4 * (u - 1))
                    elif later(g):
                        after(pe, "f_chain", g - 1, 4 * (u + 3))
                    for t in range(TG):
                        last = mm(fe[:, u % 2, 2 * t * D:2 * (t + 1) * D], xn2T[:, t * P:t * P + P],
                                  w_e0[:, E + 2 * u * D:E + 2 * (u + 1) * D])
                    last.then_inc(S["f_e_ps"], 1)
                if s == 10:
                    after(pe, "f_w", g, TG)
                    for t in range(TG):
                        last = turn(fa[0:E, t * P:t * P + P], w_tok0[:, t, :])
                    last.then_inc(S["f_wT_ps"], 1)
                if s == 12:
                    after(pe, "f_wT", g, 1)
                    for t in range(TG):
                        last = mm(fa[:, t * D:t * D + D], wT0[:, t * P:t * P + P], be0[:, :])
                    last.then_inc(S["f_b_ps"], 1)

            def attn(g, s):
                if s == 0:
                    if later(g):
                        after(pe, "a_x2", g - 1, TG)
                    else:
                        mm(bs[:, 1, 0:D], bv_bc[:, 1, :], w1T[:, 3, :]).then_inc(S["i_wps"], 1)
                        pe.wait_ge(S["i_bias"], 2)
                    for b in range(NB):
                        for h in range(2):
                            last = mm(bs[SEQ * h:SEQ * h + SEQ, 0, b * D:b * D + D], ctxT[:, b * SEQ:b * SEQ + SEQ],
                                      w1T[:, 2, :])
                    last.then_inc(S["a_v_ps"], 1)
                if s == 1:
                    after(pe, "n3_xn", g, TG)
                    turn2(bm, xn["n3"]).then_inc(S["a_xnT_ps"], 1)
                if s == 2:
                    after(pe, "a_xnT", g, 1)
                    mm(bm[:, 0:TG * P], w1T[:, 0, :], xn3T[:, :]).then_inc(S["a_q_ps"], 1)
                if s in (3, 6):
                    t = s // 6
                    if t == 0:
                        after(pe, "a_q", g, 1)
                        after(pe, "a_v", g, TG)
                    after(pe, "a_kx", g, 2 * t + 2)
                    for c in range(2):
                        if t == 1:
                            after(pe, "a_pT", g, c + 1)
                        for b in range(2):
                            q = t * P + b * SEQ
                            last = mm(bs[SEQ * b:SEQ * b + SEQ, c, :], q1T[:, q:q + SEQ],
                                      kx[:, 2 * t + b, (H // 2) * c:(H // 2) * (c + 1), :])
                        last.then_inc(S["a_s_ps"], 1)
                if s in (4, 9):
                    t = s // 9
                    for c in range(2):
                        after(pe, "a_p", g, 2 * t + c + 1)
                        for j in range(4):
                            last = turn(bs[:, c, j * P:j * P + P],
                                        p1[:, 8 * c + 2 * j:8 * c + 2 * j + 2, :].rearrange("p h k -> p (h k)"))
                        last.then_inc(S["a_pT_ps"], 1)
                if s in (5, 10):
                    t = s // 10
                    after(pe, "a_rE", g, 2 * t + 2)
                    if t == 1:
                        after(pe, "a_x2", g, 1)
                    for m in range(2):
                        last = turn(bm[:, m * P:m * P + P],
                                    rE[:, 4 * m:4 * m + 4, :, :, :].rearrange("p j b h d -> p (j b h d)"))
                    last.then_inc(S["a_rT_ps"], 1)
                if s in (7, 11):
                    t = s // 11
                    after(pe, "a_rT", g, t + 1)
                    after(pe, "a_pT", g, 2 * t + 2)
                    for m in range(2):
                        for j in range(4):
                            last = mm(bm[32 * j:32 * j + 32, m * P:m * P + P],
                                      vx[:, t, 4 * m + j, :, :].rearrange("p b c -> p (b c)"), p1T[:, 4 * m + j, :],
                                      tile_position=(0, 32 * j))
                    last.then_inc(S["a_y_ps"], 1)
                if s in (8, 12):
                    t = s // 12
                    after(pe, "a_y", g, t + 1)
                    for m in range(2):
                        last = mm(bm[:, 0:D], yT[:, m, :], wpE[:, m, :], start=(m == 0), stop=(m == 1))
                    last.then_inc(S["a_o_ps"], 1)

            def moe(g, s):
                if s == 1:
                    if later(g):
                        after(pe, "m_out", g - 1, 1)
                    after(pe, "n4_xn", g, TG)
                    turn2(bc[:, 0, :], xn["n4"]).then_inc(S["m_xnT_ps"], 1)
                if s == 2:
                    if isinstance(g, int) and g == 0:
                        pe.wait_ge(S["w_exp1"], 16 * 4)
                    after(pe, "m_xnT", g, 1)
                    for t in range(TG):
                        last = mm(bc[:, 1, t * E:t * E + E], xn4T[:, t * P:t * P + P], w_r1[:, :])
                    last.then_inc(S["m_r_ps"], 1)
                if s == 3:
                    after(pe, "m_oh", g, TG)
                    if later(g):
                        after(pe, "m_macc", g - 1, 2)
                    mm(bc[:, 0, 0:E], tri[:, :], oh1[:, 0, :], stop=False)
                    mm(bc[:, 0, 0:E], ones_bf[:, :], macc[:, :], start=False)
                    mm(bc[:, 0, E:2 * E], tri[:, :], oh1[:, 1, :], stop=False)
                    mm(bc[:, 0, E:2 * E], ones_bf[:, :], oh1[:, 0, :], start=False, stop=False)
                    mm(bc[:, 0, E:2 * E], ones_bf[:, :], macc[:, :], start=False).then_inc(S["m_c_ps"], 1)
                if s == 4:
                    after(pe, "m_kw", g, 1)
                    after(pe, "m_xg", g, TG)
                    turn2(bc[:, 1, :], xg).then_inc(S["m_xgT_ps"], 1)
                    after(pe, "m_w", g, TG)
                    for t in range(TG):
                        last = turn(bc[0:E, 0, t * P:t * P + P], w_tok1[:, t, :])
                    last.then_inc(S["m_wT_ps"], 1)
                if 5 <= s < 5 + NU:
                    u = s - 5
                    if u == 0:
                        after(pe, "m_wT", g, 1)
                        after(pe, "m_xgT", g, 1)
                    if u >= 2:
                        after(pe, "m_h", g, 2 * (u - 1))
                    for e in (2 * u, 2 * u + 1):
                        last = mm(bc[:, u % 2, TG * P * (e % 2):TG * P * (e % 2 + 1)], w_up[:, e, :], xgT[:, :])
                    last.then_inc(S["m_h_ps"], 1)
                if 9 <= s < 9 + NU:
                    u = s - 9
                    if u < 2:
                        after(pe, "m_h", g, E - 2 + 2 * u)
                    else:
                        after(pe, "m_chain", g, 4 * (u - 1))
                    for t in range(TG):
                        for e in (2 * u, 2 * u + 1):
                            last = mm(bc[:, u % 2, (2 * t + e % 2) * D:(2 * t + e % 2 + 1) * D],
                                      hT[:, e, t * P:t * P + P], w_dn[:, e, :])
                    last.then_inc(S["m_e_ps"], 1)
                if s == 13:
                    after(pe, "m_chain", g, 4 * (NU - 1))
                    for t in range(TG):
                        last = mm(bc[:, 0, t * D:t * D + D], wT1[:, t * P:t * P + P], be1[:, :])
                    last.then_inc(S["m_b_ps"], 1)

            run(pe, ORDER["tensor"], front, attn, moe)


_INS = ['x', 'ctx_1024', 'g_xattn', 'g_ffn', 'L0_xattn_Wk', 'L0_xattn_Wv', 'L0_xattn_bv', 'L0_xattn_Wq', 'L0_xattn_bq',
        'L0_xattn_Wo', 'L0_xattn_bo', 'L0_ffn_We', 'L0_ffn_be', 'L0_ffn_Wg', 'L0_ffn_bg', 'L1_xattn_Wq',
        'L1_xattn_bq', 'L1_xattn_Wk', 'L1_xattn_bk', 'L1_xattn_Wv', 'L1_xattn_bv', 'L1_xattn_Wp', 'L1_xattn_bp',
        'L1_ffn_Wr', 'L1_ffn_br', 'L1_ffn_W1', 'L1_ffn_b1', 'L1_ffn_W2', 'L1_ffn_b2']


def kernel(**inputs):
    import numpy as _np
    import concourse.bacc as _bacc
    from concourse import mybir as _mybir
    from concourse.bass_utils import run_bass_kernel_spmd as _run

    nc = _bacc.Bacc("TRN2", target_bir_lowering=False, num_devices=1)
    arrays, aps = {}, {}
    for name in _INS:
        v = _np.ascontiguousarray(inputs[name])
        arrays[f"in_{name}_dram"] = v
        aps[name] = nc.dram_tensor(f"in_{name}_dram", v.shape, _mybir.dt.from_np(v.dtype), kind="ExternalInput").ap()
    out = nc.dram_tensor("out_0_dram", inputs["x"].shape, _mybir.dt.float32, kind="ExternalOutput").ap()
    build_program(nc, aps, out)
    r = _run(nc, [arrays], core_ids=[0])
    return r.results[0]["out_0_dram"]
```

```python
from contextlib import ExitStack

import concourse.bass as bass
from concourse import mybir

F32 = mybir.dt.float32
BF16 = mybir.dt.bfloat16
U32 = mybir.dt.uint32
ALU = mybir.AluOpType
ACT = mybir.ActivationFunctionType
AX_X = mybir.AxisListType.X

P = 128
D = 128
SEQ = 64
TG = 2
NB = TG * P // SEQ
E = 8
H = 16
DH = D // H
NJ = H // 2
EPS = 1e-5
SCALE0 = float(D) ** -0.5
SCALE1 = float(DH) ** -0.5
NU = E // 2
BARRED = -float(2 ** 100)
ORDER = {
    "tensor": """
m9 m10 a10 f9 a11 f10 f11 m11 f12 a12 m12 f0 a0 f1 a1 m1 a2 m2 a3 m3 f2 m4 f3 m5 m6 a4 f4 a5 f5 a6 m7 a7 m8
a8 f6 a9 f7 f8
""".split(),
    "vector": """
f9 f10 a11 f11 f12 m11 f13 f0 a12 a0 m12 m0 f1 a1 m1 m2 m3 a3 f2 f3 a4 f4 f5 a6 a7 f6 a8 a9 f7 f8
""".split(),
    "scalar": """
a10 f10 f0 a0 a1 m1 a2 f1 m2 m3 f2 m4 a3 f3 f4 a4 a5 m5 m6 m7 a6 m8 f6 a9 f7
""".split(),
    "gpsimd": """
f0 a0 m0 k1 f5 m1 a2 k2 k3 k4
""".split(),
}

LATE = """
f9 m9 a10 f10 m10 a11 f11 m11 a12 f12 m12 f13
""".split()


def behind(step):
    return {"f": 0, "k": 0, "a": 1, "m": 2}[step[0]] + (step in LATE)


LAST_BEHIND = max(behind(step) for order in ORDER.values() for step in order)

NORM = {"_stats": TG, "_mv": TG, "_eps": 1, "_rstd": 1, "_xn": TG}
PER_GROUP = {
    "x_loaded": 16, "ctx_loaded": 16, "out_stored": 16,
    **{n + k: c for n in ("n1", "n2", "n3", "n4") for k, c in NORM.items()},
    "f_ctxT_ps": 1, "f_ctxT": 1, "f_xnT_ps": 1, "f_xnT": 1, "f_q_ps": 1, "f_q": 1, "f_v_ps": 1, "f_v": 1,
    "f_s_ps": 1, "f_max": 2, "f_negmax": 1, "f_p": 2 * TG, "f_rinv": 1, "f_pT_ps": 1, "f_pT": 1,
    "f_pv_ps": 1, "f_x1": TG, "f_xn2T_ps": 1, "f_xn2T": 1,
    "f_r_ps": 1, "f_lg": 1, "f_neg": 1, "f_top": TG, "f_idx": TG, "f_idxf": 1, "f_oh1": TG, "f_oh": TG,
    "f_ex": TG, "f_sel": TG, "f_rsum": 1, "f_w": TG, "f_e_ps": NU, "f_chain": NU * 4, "f_wT_ps": 1, "f_wT": 1,
    "f_b_ps": 1, "f_out": 1,
    "a_k_ps": 1, "a_k": 1, "a_v_ps": 1, "a_v": 2 * TG, "a_kx": NB, "a_xb": 1, "a_xnT_ps": 1, "a_xnT": 1,
    "a_q_ps": 1, "a_q": 1, "a_s_ps": 2 * TG, "a_max": 2 * TG, "a_sub": 2 * TG, "a_p": 2 * TG,
    "a_pT_ps": 2 * TG, "a_pT": 2 * TG, "a_sum": 2 * TG, "a_rinv": TG, "a_rE": TG, "a_rT_ps": TG, "a_rT": TG, "a_y_ps": TG, "a_y": TG,
    "a_o_ps": TG, "a_x2": TG,
    "m_x2": 1, "m_xnT_ps": 1, "m_xnT": 1, "m_r_ps": 1, "m_lg": 1, "m_neg": 1, "m_top": TG, "m_idx": TG,
    "m_idxf": 1, "m_se": TG, "m_oh": TG, "m_c_ps": 1, "m_kw": 1, "m_gate": 1, "m_gw": 1, "m_macc": 2,
    "m_xg": TG, "m_xgT_ps": 1, "m_xgT": 1, "m_kT": 1, "m_nT": 1, "m_h_ps": NU, "m_h": E,
    "m_e_ps": 2 * TG, "m_out": TG,
}
SETUP = ["w_attn0", "w_exp0", "w_attn1", "w_exp1", "w_gates", "w_rows", "w_cols0", "w_cols1", "i_zero", "i_ident", "i_one", "i_sel",
         "i_iota", "i_dve", "i_conv", "i_tanh", "i_ps", "i_ev", "i_wps", "i_wev", "i_bias",
         "i_bar"]


def build_program(nc, a, out):
    n_tok = a["x"].shape[0] * a["x"].shape[1]
    NG = n_tok // (TG * P)
    CAP = n_tok // E
    x_v = a["x"].rearrange("b s d -> (b s) d").rearrange("(g t p) d -> g p t d", t=TG, p=P)
    c_v = a["ctx_1024"].rearrange("b s d -> (b s) d").rearrange("(g t p) d -> g p t d", t=TG, p=P)
    o_v = out.rearrange("b s d -> (b s) d").rearrange("(g t p) d -> g p t d", t=TG, p=P)

    with ExitStack() as ctx:
        def sb(name, shape, dt=F32):
            return ctx.enter_context(nc.sbuf_tensor(name, shape, dt))

        def psum(name, shape, dt=F32):
            return ctx.enter_context(nc.psum_tensor(name, shape, dt))

        S = {n: ctx.enter_context(nc.semaphore(n)) for n in list(PER_GROUP) + SETUP}

        def after(eng, name, g, n):
            eng.wait_ge(S[name], g * PER_GROUP[name] + n)

        zero = sb("zero", [P, P])
        ident = sb("ident", [P, P])
        ones = sb("ones", [P, P])
        tri_f = sb("tri_f", [P, P])
        tri = sb("tri", [P, P], BF16)
        ones_bf = sb("ones_bf", [P, P], BF16)
        head_mask = sb("head_mask", [P, H])
        pair_mask = sb("pair_mask", [P, 2])
        bar_f = sb("bar_f", [E, E, P])
        bar = sb("bar", [E, E, P], BF16)
        iota_u = sb("iota_u", [P, E], U32)
        iota = sb("iota", [P, E])
        half_neg = sb("half_neg", [P, TG])
        eps = sb("eps", [P, TG])
        w0 = sb("w0", [P, 4, D])
        w1 = sb("w1", [P, 4, D])
        w_e0 = sb("w_e0", [P, E + E * D])
        w_r1 = sb("w_r1", [P, E])
        w_up = sb("w_up", [P, E, D])
        w_dn = sb("w_dn", [P, E, D])
        be0 = sb("be0", [E, D])
        be1 = sb("be1", [E, D])
        b_up_rows = sb("b_up_rows", [E, D])
        cols = sb("cols", [P, 5])
        bo_bc = sb("bo_bc", [P, D])
        bp_bc = sb("bp_bc", [P, D])
        rb_bc = sb("rb_bc", [P, 2, E])
        g_bc = sb("g_bc", [P, 4])
        tg = sb("tg", [P, 4])
        wqk = sb("wqk", [P, D])
        bqk = sb("bqk", [P, 1])
        woT = sb("woT", [P, D])
        wvo = sb("wvo", [P, D])
        bv_bc = sb("bv_bc", [P, 2, P])
        vo_bias = sb("vo_bias", [P, D])
        w1T = sb("w1T", [P, 4, D])
        wp_gap = sb("wp_gap", [P, 2, 4, 2, 2 * DH])
        wpE = sb("wpE", [P, 2, D])
        p_bias = sb("p_bias", [P, D])
        b_upT = sb("b_upT", [P, E])
        x_in = sb("x_in", [P, TG, D])
        ctx_in = sb("ctx_in", [P, TG, D])
        wait_carrier = sb("wait_carrier", [P, 1])
        stats = {n: sb(n + "_st", [P, TG, 6]) for n in ("n1", "n2", "n3", "n4")}
        mv = {n: sb(n + "_mvb", [P, TG, 2]) for n in stats}
        ve = {n: sb(n + "_ve", [P, TG]) for n in stats}
        rstd = {n: sb(n + "_rs", [P, TG]) for n in stats}
        xn = {n: sb(n + "_xnb", [P, TG, D]) for n in stats}
        ctxT = sb("ctxT", [P, TG * P])
        xnT = sb("xnT", [P, TG * P])
        qT = sb("qT", [P, TG * P])
        vo = sb("vo", [P, TG, D])
        mx0 = sb("mx0", [P, TG])
        nmx0 = sb("nmx0", [P, TG])
        p0 = sb("p0", [P, TG, P])
        rs0 = sb("rs0", [P, TG])
        ri0 = sb("ri0", [P, TG])
        p0T = sb("p0T", [P, TG, P])
        x1 = sb("x1", [P, TG, D])
        xn2T = sb("xn2T", [P, TG * P])
        lg0 = sb("lg0", [P, TG, E])
        top0 = sb("top0", [P, TG, 8])
        idx0 = sb("idx0", [P, TG, 8], U32)
        idx0f = sb("idx0f", [P, TG, 2])
        neg0 = sb("neg0", [P, TG])
        ex0 = sb("ex0", [P, TG, E])
        oh0a = sb("oh0a", [P, TG, E])
        oh0 = sb("oh0", [P, TG, E])
        sel0 = sb("sel0", [P, TG, E])
        sum0 = sb("sum0", [P, TG])
        rsum0 = sb("rsum0", [P, TG])
        w_tok0 = sb("w_tok0", [P, TG, E])
        wT0 = sb("wT0", [E, TG * P])
        acc0 = sb("acc0", [P, TG, D])
        x_mid = sb("x_mid", [P, TG, D])
        k1T = sb("k1T", [P, NB, SEQ])
        kx = sb("kx", [P, NB, H, SEQ])
        vx = sb("vx", [P, TG, 2 * D + 2 * DH])
        xb = sb("xb", [P, TG, D])
        xn3T = sb("xn3T", [P, TG * P])
        q1T = sb("q1T", [P, TG * P])
        mx1 = sb("mx1", [P, H])
        p1 = sb("p1", [P, H, SEQ])
        p1T = sb("p1T", [P, NJ, P])
        sum1 = sb("sum1", [P, H])
        ri1 = sb("ri1", [P, NJ, 2, 2])
        rE = sb("rE", [P, 4 * NJ, DH])
        rT = sb("rT", [P, 2, P])
        yT = sb("yT", [P, 2, P])
        x2 = sb("x2", [P, TG, D])
        xn4T = sb("xn4T", [P, TG * P])
        lg1 = sb("lg1", [P, TG, E])
        top1 = sb("top1", [P, TG, 8])
        idx1 = sb("idx1", [P, TG, 8], U32)
        idx1f = sb("idx1f", [P, TG, 1])
        neg1 = sb("neg1", [P, TG])
        ex1 = sb("ex1", [P, TG, E])
        se1 = sb("se1", [P, TG])
        gate1 = sb("gate1", [P, TG])
        oh1 = sb("oh1", [P, TG, E], BF16)
        macc = sb("macc", [P, E], BF16)
        kw1 = sb("kw1", [P, TG, E])
        gw1 = sb("gw1", [P, TG])
        xg = sb("xg", [P, TG, D])
        xgT = sb("xgT", [P, TG * P])
        kT1 = sb("kT1", [E, TG * P])
        nT1 = sb("nT1", [E, TG * P], BF16)
        hT = sb("hT", [P, E, TG * P])
        o_sb = sb("o_sb", [P, TG, D])
        fa = psum("fa", [P, 512])
        fe = psum("fe", [P, 2, 512])
        bs = psum("bs", [P, 2, 512])
        bm = psum("bm", [P, 512])
        bc = psum("bc", [P, 2, 512])

        def run(eng, order, front, attn, moe, keys=None):
            def steps(i):
                for step in order:
                    if isinstance(i, int) and not 0 <= i - behind(step) < NG:
                        continue
                    g, s = i - behind(step), int(step[1:])
                    if step[0] == "f":
                        front(g, s)
                    if step[0] == "k" and keys is not None:
                        keys(g, s)
                    if step[0] == "a":
                        attn(g, s)
                    if step[0] == "m":
                        moe(g, s)

            for i in range(LAST_BEHIND + 1):
                steps(i)
            with eng.Fori(LAST_BEHIND + 1, NG) as i:
                steps(i)
            for i in range(NG, NG + LAST_BEHIND):
                steps(i)

        def later(g):
            return not (isinstance(g, int) and g == 0)

        block = ctx.enter_context(nc.Block())

        @block.sync
        def _(sp):
            def load(g):
                if later(g):
                    after(sp, "f_x1", g - 1, TG)
                sp.dma_start(x_in[:, :, :], x_v[g]).then_inc(S["x_loaded"], 16)
                sp.dma_start(ctx_in[:, :, :], c_v[g]).then_inc(S["ctx_loaded"], 16)

            def store(g):
                after(sp, "m_out", g, TG)
                sp.dma_start(o_v[g], o_sb[:, :, :]).then_inc(S["out_stored"], 16)

            load(0)
            for n, name in enumerate(("Wq", "Wk", "Wv", "Wo")):
                sp.dma_start(w0[:, n, :], a["L0_xattn_" + name]).then_inc(S["w_attn0"], 16)
            sp.dma_start(w_e0[:, 0:E], a["L0_ffn_Wg"]).then_inc(S["w_exp0"], 16)
            sp.dma_start(w_e0[:, E:].rearrange("p (e o) -> p e o", e=E),
                         a["L0_ffn_We"].rearrange("e d o -> d e o")).then_inc(S["w_exp0"], 16)
            sp.dma_start(be0[:, :], a["L0_ffn_be"]).then_inc(S["w_exp0"], 16)
            load(1)
            sp.dma_start(w_r1[:, :], a["L1_ffn_Wr"]).then_inc(S["w_exp1"], 16)
            sp.dma_start(w_up[:, :, :], a["L1_ffn_W1"].rearrange("e d f -> d e f")).then_inc(S["w_exp1"], 16)
            sp.dma_start(w_dn[:, :, :], a["L1_ffn_W2"].rearrange("e f d -> f e d")).then_inc(S["w_exp1"], 16)
            sp.dma_start(be1[:, :], a["L1_ffn_b2"]).then_inc(S["w_exp1"], 16)
            load(2)
            load(3)
            with sp.Fori(0, NG - 4) as g:
                store(g)
                load(g + 4)
            for g in range(NG - 4, NG):
                store(g)
            sp.wait_ge(S["out_stored"], 16 * NG)

        @block.scalar
        def _(act):
            def load_column(n, name, sem):
                act.dma_start(cols[:, n:n + 1], a[name].rearrange("(p o) -> p o", o=1)).then_inc(S[sem], 16)

            load_column(0, "L0_xattn_bq", "w_cols0")
            load_column(1, "L0_xattn_bv", "w_cols0")
            for n, src in enumerate((a["g_xattn"], a["g_ffn"])):
                act.dma_start(g_bc[:, 2 * n:2 * n + 2], src.partition_broadcast(P)).then_inc(S["w_gates"], 16)
            for n, name in enumerate(("Wq", "Wk", "Wv", "Wp")):
                act.dma_start(w1[:, n, :], a["L1_xattn_" + name]).then_inc(S["w_attn1"], 16)
            for n, name in enumerate(("L1_xattn_bq", "L1_xattn_bk", "L1_xattn_bv")):
                load_column(2 + n, name, "w_cols1")
            act.wait_ge(S["w_gates"], 16 * 2)
            nc.scalar.activation(tg[:, :], g_bc[:, :], ACT.Tanh).then_inc(S["i_tanh"], 1)

            def copy(dst, src, name, bias=None):
                if bias is None:
                    return nc.scalar.copy(dst, src).then_inc(S[name], 1)
                return nc.scalar.activation(dst, src, ACT.Identity, bias=bias).then_inc(S[name], 1)

            def front(g, s):
                if s == 0:
                    if later(g):
                        after(act, "a_v_ps", g - 1, 1)
                    after(act, "f_ctxT_ps", g, 1)
                    copy(ctxT[:, :], fa[:, 0:TG * P], "f_ctxT")
                if s == 1:
                    after(act, "f_xnT_ps", g, 1)
                    copy(xnT[:, :], fe[:, 0, 0:TG * P], "f_xnT")
                    if later(g):
                        after(act, "a_kx", g - 1, NB)
                    if isinstance(g, int) and g == 0:
                        act.wait_ge(S["w_cols1"], 16 * 3)
                    after(act, "a_k_ps", g, 1)
                    copy(k1T[:, :, :], fa[:, 0:TG * P].rearrange("p (b k) -> p b k", b=NB), "a_k", bias=cols[:, 3:4])
                if s == 2:
                    after(act, "f_q_ps", g, 1)
                    copy(qT[:, :], fa[:, 0:TG * P], "f_q", bias=bqk[:, 0:1])
                if s == 3:
                    after(act, "f_negmax", g, 1)
                    for t in range(TG):
                        for b in range(2):
                            r = slice(SEQ * b, SEQ * b + SEQ)
                            nc.scalar.activation(p0[r, t, r], fa[r, t * P + SEQ * b:t * P + SEQ * b + SEQ], ACT.Exp,
                                                 bias=nmx0[r, t:t + 1], scale=SCALE0,
                                                 accum_out=rs0[r, t:t + 1]).then_inc(S["f_p"], 1)
                if s == 4:
                    after(act, "f_pT_ps", g, 1)
                    copy(p0T[:, :, :], fe[:, 0, 0:TG * P].rearrange("p (t q) -> p t q", t=TG), "f_pT")
                if s == 6:
                    after(act, "f_xn2T_ps", g, 1)
                    copy(xn2T[:, :], fe[:, 0, 0:TG * P], "f_xn2T")
                if s == 7:
                    after(act, "f_neg", g, 1)
                    for t in range(TG):
                        nc.scalar.activation(ex0[:, t, :], lg0[:, t, :], ACT.Exp,
                                             bias=neg0[:, t:t + 1]).then_inc(S["f_ex"], 1)
                if s == 10:
                    after(act, "f_wT_ps", g, 1)
                    copy(wT0[:, :], fa[0:E, 0:TG * P], "f_wT")

            def attn(g, s):
                if s == 0:
                    after(act, "a_v_ps", g, 1)
                    for t in range(TG):
                        for h in range(2):
                            nc.scalar.activation(
                                vx[:, t, 0:2 * D].rearrange("p (j b h d) -> p h b j d", j=NJ, b=2, h=2)[:, h],
                                bs[:, 0, t * 2 * D:(t + 1) * 2 * D].rearrange("p (b j h d) -> p h b j d", b=2, j=NJ,
                                                                               h=2)[:, h],
                                ACT.Copy, scale=pair_mask[:, h:h + 1]).then_inc(S["a_v"], 1)
                if s == 1:
                    after(act, "a_xnT_ps", g, 1)
                    copy(xn3T[:, :], bm[:, 0:TG * P], "a_xnT")
                if s == 2:
                    after(act, "a_q_ps", g, 1)
                    copy(q1T[:, :], bm[:, 0:TG * P], "a_q", bias=cols[:, 2:3])
                if s in (3, 6):
                    t = s // 6
                    for c in range(2):
                        hs = slice(c * H // 2, (c + 1) * H // 2)
                        after(act, "a_sub", g, 2 * t + c + 1)
                        nc.scalar.activation(p1[:, hs, :], p1[:, hs, :], ACT.Exp, scale=SCALE1).then_inc(S["a_p"], 1)
                if s in (4, 9):
                    t = s // 9
                    for c in range(2):
                        after(act, "a_pT_ps", g, 2 * t + c + 1)
                        copy(p1T[:, 4 * c:4 * c + 4, :], bs[:, c, :].rearrange("p (j q) -> p j q", j=4), "a_pT")
                if s in (5, 10):
                    t = s // 10
                    after(act, "a_rT_ps", g, t + 1)
                    copy(rT[:, :, :], bm[:, 0:2 * P].rearrange("p (m q) -> p m q", m=2), "a_rT")

            def moe(g, s):
                if s == 1:
                    after(act, "m_xnT_ps", g, 1)
                    copy(xn4T[:, :], bc[:, 0, 0:TG * P], "m_xnT")
                if s == 2:
                    after(act, "m_neg", g, 1)
                    for t in range(TG):
                        nc.scalar.activation(ex1[:, t, :], lg1[:, t, :], ACT.Exp, bias=neg1[:, t:t + 1],
                                             accum_out=se1[:, t:t + 1]).then_inc(S["m_se"], 1)
                if s == 3:
                    after(act, "m_gate", g, 1)
                    for t in range(TG):
                        nc.scalar.activation(xg[:, t, :], xn["n4"][:, t, :], ACT.Copy,
                                             scale=gate1[:, t:t + 1]).then_inc(S["m_xg"], 1)
                if s == 4:
                    after(act, "m_xgT_ps", g, 1)
                    copy(xgT[:, :], bc[:, 1, 0:TG * P], "m_xgT")
                    nc.scalar.activation(nT1[:, :], bc[0:E, 1, TG * P:2 * TG * P], ACT.Identity, bias=ones[0:E, 0:1],
                                         scale=-1.0).then_inc(S["m_nT"], 1)
                    copy(kT1[:, :], bc[0:E, 1, TG * P:2 * TG * P], "m_kT")
                if 5 <= s < 5 + NU:
                    u = s - 5
                    if u == 0 and later(g):
                        after(act, "m_e_ps", g - 1, 2 * TG)
                    after(act, "m_h_ps", g, u + 1)
                    for e in (2 * u, 2 * u + 1):
                        nc.scalar.activation(hT[:, e, :], bc[:, u % 2, TG * P * (e % 2):TG * P * (e % 2 + 1)], ACT.Relu,
                                             bias=b_upT[:, e:e + 1]).then_inc(S["m_h"], 1)

            run(act, ORDER["scalar"], front, attn, moe)

        @block.gpsimd
        def _(pool):
            nc.gpsimd.memset(zero[:, :], 0.0).then_inc(S["i_zero"], 1)
            nc.gpsimd.memset(ones[:, :], 1.0).then_inc(S["i_one"], 1)
            nc.gpsimd.iota(iota_u[:, :], pattern=[[1, E]], base=0, channel_multiplier=0).then_inc(S["i_iota"], 1)
            nc.gpsimd.memset(half_neg[:, :], -0.5).then_inc(S["i_one"], 1)
            nc.gpsimd.memset(eps[:, :], EPS).then_inc(S["i_one"], 1)
            pool.dma_start(bo_bc[:, :], a["L0_xattn_bo"].partition_broadcast(P)).then_inc(S["w_rows"], 16)
            for n, name in enumerate(("L0_ffn_bg", "L1_ffn_br")):
                pool.dma_start(rb_bc[:, n, :], a[name].partition_broadcast(P)).then_inc(S["w_rows"], 16)
            pool.dma_start(bp_bc[:, :], a["L1_xattn_bp"].partition_broadcast(P)).then_inc(S["w_rows"], 16)
            pool.dma_start(b_up_rows[:, :], a["L1_ffn_b1"]).then_inc(S["w_rows"], 16)
            pool.wait_ge(S["i_zero"], 1)
            nc.gpsimd.affine_select(out=ident[:, :], in_=zero[:, :], compare_op=ALU.not_equal, fill=1.0, base=0,
                                    pattern=[[-1, P]], channel_multiplier=1).then_inc(S["i_ident"], 1)
            pool.wait_ge(S["i_one"], 3)
            nc.gpsimd.affine_select(out=tri_f[:, :], in_=ones[:, :], compare_op=ALU.is_ge, fill=0.0, base=0,
                                    pattern=[[1, P]], channel_multiplier=-1).then_inc(S["i_sel"], 1)
            nc.gpsimd.affine_select(out=head_mask[:, :], in_=ones[:, 0:H], compare_op=ALU.is_ge, fill=0.0, base=0,
                                    pattern=[[-DH, H]], channel_multiplier=1).then_inc(S["i_sel"], 1)
            pool.wait_ge(S["i_sel"], 2)
            nc.gpsimd.affine_select(out=head_mask[:, :], in_=head_mask[:, :], compare_op=ALU.is_ge, fill=0.0,
                                    base=DH - 1, pattern=[[DH, H]], channel_multiplier=-1).then_inc(S["i_sel"], 1)
            pool.wait_ge(S["i_sel"], 3)
            nc.gpsimd.affine_select(out=bar_f[:, :, :], in_=zero[0:E, :].unsqueeze(1).to_broadcast([E, E, P]),
                                    compare_op=ALU.not_equal, fill=BARRED, base=0, pattern=[[-1, E], [0, P]],
                                    channel_multiplier=1).then_inc(S["i_sel"], 1)

            def rstd_of(n, g):
                after(pool, n + "_mv", g, TG)
                nc.gpsimd.tensor_tensor(ve[n][:, :], mv[n][:, :, 1], eps[:, :], ALU.add).then_inc(S[n + "_eps"], 1)
                after(pool, n + "_eps", g, 1)
                nc.gpsimd.tensor_tensor(rstd[n][:, :], ve[n][:, :], half_neg[:, :], ALU.pow)\
                 .then_inc(S[n + "_rstd"], 1)

            def spread_keys(g, b):
                nc.gpsimd.tensor_tensor(kx[:, b, :, :], k1T[:, b, :].unsqueeze(1).to_broadcast([P, H, SEQ]),
                                        head_mask[:, :].unsqueeze(2).to_broadcast([P, H, SEQ]),
                                        ALU.mult).then_inc(S["a_kx"], 1)

            def front(g, s):
                if s == 0:
                    rstd_of("n1", g)
                if s == 5:
                    rstd_of("n2", g)

            def attn(g, s):
                if s == 0:
                    rstd_of("n3", g)
                if s == 2:
                    if later(g):
                        after(pool, "a_x2", g - 1, TG)
                    if isinstance(g, int) and g == 0:
                        pool.wait_ge(S["i_bias"], 2)
                    after(pool, "f_out", g, 1)
                    nc.gpsimd.tensor_tensor(xb[:, :, :], x_mid[:, :, :],
                                            p_bias[:, :].unsqueeze(1).to_broadcast([P, TG, D]),
                                            ALU.add).then_inc(S["a_xb"], 1)

            def keys(g, s):
                if s in (1, 3):
                    if later(g):
                        after(pool, "a_s_ps", g - 1, s + 1)
                    after(pool, "a_k", g, 1)
                spread_keys(g, s - 1)

            def moe(g, s):
                if s == 0:
                    rstd_of("n4", g)
                if s == 1:
                    if later(g):
                        after(pool, "out_stored", g - 1, 16)
                    after(pool, "a_x2", g, TG)
                    nc.gpsimd.tensor_tensor(o_sb[:, :, :], x2[:, :, :], zero[:, :].unsqueeze(1).to_broadcast([P, TG, D]),
                                            ALU.add).then_inc(S["m_x2"], 1)

            run(pool, ORDER["gpsimd"], front, attn, moe, keys)

        @block.vector
        def _(dve):
            V = nc.vector
            V.memset(pair_mask[:, :], 0.0).then_inc(S["i_dve"], 1)
            V.memset(vx[:, :, 2 * D:], 0.0).then_inc(S["i_dve"], 1)
            V.memset(p0[:, :, :], 0.0).then_inc(S["i_dve"], 1)
            V.memset(macc[:, :], 0.0).then_inc(S["i_dve"], 1)
            dve.wait_ge(S["i_dve"], 4)
            for b in range(2):
                r = slice(SEQ * b, SEQ * b + SEQ)
                V.memset(pair_mask[r, b:b + 1], 1.0).then_inc(S["i_dve"], 1)
            dve.wait_ge(S["i_iota"], 1)
            V.tensor_copy(iota[:, :], iota_u[:, :]).then_inc(S["i_conv"], 1)
            dve.wait_ge(S["i_sel"], 3)
            V.tensor_copy(tri[:, :], tri_f[:, :]).then_inc(S["i_conv"], 1)
            V.tensor_copy(ones_bf[:, :], ones[:, :]).then_inc(S["i_conv"], 1)
            dve.wait_ge(S["w_cols0"], 16 * 2)
            V.tensor_scalar(bv_bc[:, 0, :], ones[:, :], cols[:, 1:2], None, ALU.mult).then_inc(S["i_conv"], 1)
            dve.wait_ge(S["i_ps"], 1)
            V.tensor_copy(woT[:, :], bc[:, 0, 0:D]).then_inc(S["i_ev"], 1)
            V.tensor_copy(wqk[:, :], bc[:, 0, D:2 * D]).then_inc(S["i_ev"], 1)
            V.tensor_copy(bqk[:, :], bc[:, 0, 2 * D:2 * D + 1]).then_inc(S["i_ev"], 1)
            dve.wait_ge(S["i_wps"], 1)
            V.tensor_copy(w1T[:, :, :], bs[:, 0, :].rearrange("p (n d) -> p n d", n=4)).then_inc(S["i_wev"], 1)
            def finish_block0():
                dve.wait_ge(S["i_tanh"], 1)
                dve.wait_ge(S["i_ps"], 2)
                V.tensor_scalar(wvo[:, :], bc[:, 1, 0:D], tg[:, 0:1], None, ALU.mult).then_inc(S["i_ev"], 1)
                dve.wait_ge(S["w_rows"], 16 * 5)
                V.tensor_tensor(vo_bias[:, :], bc[:, 1, D:2 * D], bo_bc[:, :], ALU.add).then_inc(S["i_bias"], 1)
                dve.wait_ge(S["i_bias"], 1)
                V.tensor_scalar(vo_bias[:, :], vo_bias[:, :], tg[:, 0:1], None, ALU.mult).then_inc(S["i_ev"], 1)
                dve.wait_ge(S["w_cols1"], 16 * 3)
                V.tensor_scalar(bv_bc[:, 1, :], ones[:, :], cols[:, 4:5], None, ALU.mult).then_inc(S["i_conv"], 1)
                V.memset(wp_gap[:, :, :, 1, :], 0.0).then_inc(S["i_conv"], 1)
                V.tensor_copy(wp_gap[:, :, :, 0, :],
                              w1[:, 3, :].rearrange("p (m j c) -> p m j c", m=2, j=4)).then_inc(S["i_conv"], 1)
                dve.wait_ge(S["i_ev"], 5)

            def finish_block1():
                dve.wait_ge(S["i_sel"], 4)
                V.tensor_copy(bar[:, :, :], bar_f[:, :, :]).then_inc(S["i_bar"], 1)
                dve.wait_ge(S["i_wps"], 2)
                V.tensor_scalar(wpE[:, :, :], bm[:, 0:2 * D].rearrange("p (m d) -> p m d", m=2), tg[:, 1:2], None,
                                ALU.mult).then_inc(S["i_wev"], 1)
                V.tensor_copy(b_upT[:, :], bm[:, 2 * D:2 * D + E]).then_inc(S["i_wev"], 1)
                dve.wait_ge(S["i_wps"], 3)
                V.tensor_tensor(p_bias[:, :], bs[:, 1, 0:D], bp_bc[:, :], ALU.add).then_inc(S["i_wev"], 1)
                dve.wait_ge(S["i_wev"], 4)
                V.tensor_scalar(p_bias[:, :], p_bias[:, :], tg[:, 1:2], None, ALU.mult).then_inc(S["i_bias"], 1)

            def norm(n, src, g):
                for t in range(TG):
                    V.bn_stats(stats[n][:, t, :], src[:, t, :]).then_inc(S[n + "_stats"], 1)
                after(dve, n + "_stats", g, TG)
                V.memset(wait_carrier[:, :], 0.0)
                for t in range(TG):
                    V.bn_aggr(mv[n][:, t, :], stats[n][:, t, :]).then_inc(S[n + "_mv"], 1)

            def norm_apply(n, src, g):
                after(dve, n + "_rstd", g, 1)
                for t in range(TG):
                    V.tensor_scalar(xn[n][:, t, :], src[:, t, :], mv[n][:, t, 0:1], rstd[n][:, t:t + 1], ALU.subtract,
                                    ALU.mult).then_inc(S[n + "_xn"], 1)

            def combine(name, g, u, acc, first, w, bank):
                for n in range(4):
                    e, t = 2 * u + n // 2, n % 2
                    if u or n >= 2:
                        after(dve, name, g, 4 * u + n - 1)
                    V.scalar_tensor_tensor(out=acc[:, t, :], in0=bank[:, (2 * t + n // 2) * D:(2 * t + n // 2 + 1) * D],
                                           scalar=w[:, t, e:e + 1], in1=(acc if e else first)[:, t, :],
                                           op0=ALU.mult, op1=ALU.add).then_inc(S[name], 1)

            def logits(k, g, bank, row, lg, neg, top):
                after(dve, k + "_r_ps", g, 1)
                V.tensor_tensor(lg[:, :, :], bank[:, 0:TG * E].rearrange("p (t e) -> p t e", t=TG),
                                rb_bc[:, row:row + 1, :].to_broadcast([P, TG, E]), ALU.add).then_inc(S[k + "_lg"], 1)
                after(dve, k + "_lg", g, 1)
                V.tensor_reduce(neg[:, :], lg[:, :, :], AX_X, ALU.max, negate=True).then_inc(S[k + "_neg"], 1)
                for t in range(TG):
                    V.max(top[:, t, :], lg[:, t, :]).then_inc(S[k + "_top"], 1)

            def places(k, g, lg, top, idx, idxf, n):
                after(dve, k + "_top", g, TG)
                V.memset(wait_carrier[:, :], 0.0)
                for t in range(TG):
                    V.max_index(idx[:, t, :], top[:, t, :], lg[:, t, :]).then_inc(S[k + "_idx"], 1)
                after(dve, k + "_idx", g, TG)
                V.tensor_copy(idxf[:, :, :], idx[:, :, 0:n]).then_inc(S[k + "_idxf"], 1)
                after(dve, k + "_idxf", g, 1)

            def front(g, s):
                if s == 0:
                    after(dve, "x_loaded", g, 16)
                    norm("n1", x_in, g)
                if s == 1:
                    norm_apply("n1", x_in, g)
                if s == 2:
                    if isinstance(g, int) and g == 0:
                        finish_block0()
                    after(dve, "f_v_ps", g, 1)
                    V.tensor_tensor(vo[:, :, :], fe[:, 1, 0:TG * D].rearrange("p (t d) -> p t d", t=TG),
                                    vo_bias[:, :].unsqueeze(1).to_broadcast([P, TG, D]), ALU.add)\
                     .then_inc(S["f_v"], 1)
                if s == 3:
                    after(dve, "f_s_ps", g, 1)
                    for b in range(2):
                        r = slice(SEQ * b, SEQ * b + SEQ)
                        V.tensor_reduce(mx0[r, :], fa[r, 0:TG * P].rearrange("p (t k) -> p t k", t=TG)[:, :, r],
                                        AX_X, ALU.max).then_inc(S["f_max"], 1)
                    after(dve, "f_max", g, 2)
                    V.tensor_scalar(nmx0[:, :], mx0[:, :], -SCALE0, None, ALU.mult).then_inc(S["f_negmax"], 1)
                if s == 4:
                    after(dve, "f_p", g, 2 * TG)
                    V.reciprocal(ri0[:, :], rs0[:, :]).then_inc(S["f_rinv"], 1)
                if s == 5:
                    after(dve, "f_rinv", g, 1)
                    after(dve, "f_pv_ps", g, 1)
                    for t in range(TG):
                        V.scalar_tensor_tensor(out=x1[:, t, :], in0=fa[:, t * D:t * D + D], scalar=ri0[:, t:t + 1],
                                               in1=x_in[:, t, :], op0=ALU.mult, op1=ALU.add)\
                         .then_inc(S["f_x1"], 1)
                    after(dve, "f_x1", g, TG)
                    norm("n2", x1, g)
                if s == 6:
                    norm_apply("n2", x1, g)
                if s == 7:
                    logits("f", g, fa, 0, lg0, neg0, top0)
                    places("f", g, lg0, top0, idx0, idx0f, 2)
                    for t in range(TG):
                        V.tensor_scalar(oh0a[:, t, :], iota[:, :], idx0f[:, t, 0:1], None, ALU.is_equal)\
                         .then_inc(S["f_oh1"], 1)
                    for t in range(TG):
                        after(dve, "f_oh1", g, t + 1)
                        V.scalar_tensor_tensor(out=oh0[:, t, :], in0=iota[:, :], scalar=idx0f[:, t, 1:2],
                                               in1=oh0a[:, t, :], op0=ALU.is_equal, op1=ALU.add)\
                         .then_inc(S["f_oh"], 1)
                if s == 8:
                    for t in range(TG):
                        after(dve, "f_oh", g, t + 1)
                        after(dve, "f_ex", g, t + 1)
                        V.tensor_tensor_reduce(sel0[:, t, :], ex0[:, t, :], oh0[:, t, :], 1.0, 0.0, ALU.mult, ALU.add,
                                               sum0[:, t:t + 1]).then_inc(S["f_sel"], 1)
                    after(dve, "f_sel", g, TG)
                    V.reciprocal(rsum0[:, :], sum0[:, :]).then_inc(S["f_rsum"], 1)
                    after(dve, "f_rsum", g, 1)
                    for t in range(TG):
                        V.tensor_scalar(w_tok0[:, t, :], sel0[:, t, :], rsum0[:, t:t + 1], tg[:, 2:3], ALU.mult,
                                        ALU.mult).then_inc(S["f_w"], 1)
                if 9 <= s < 9 + NU:
                    u = s - 9
                    if u == 0:
                        after(dve, "f_w", g, TG)
                    after(dve, "f_e_ps", g, u + 1)
                    combine("f_chain", g, u, acc0, x1, w_tok0, fe[:, u % 2, :])
                if s == 13:
                    after(dve, "f_chain", g, NU * 4)
                    if later(g):
                        after(dve, "a_xb", g - 1, 1)
                    after(dve, "f_b_ps", g, 1)
                    V.tensor_tensor(x_mid[:, :, :], fa[:, 0:TG * D].rearrange("p (t d) -> p t d", t=TG),
                                    acc0[:, :, :], ALU.add).then_inc(S["f_out"], 1)

            def attn(g, s):
                if s == 0:
                    if isinstance(g, int) and g == 0:
                        finish_block1()
                    after(dve, "f_out", g, 1)
                    norm("n3", x_mid, g)
                if s == 1:
                    norm_apply("n3", x_mid, g)
                if s in (3, 6):
                    t = s // 6
                    for c in range(2):
                        n, hs = 2 * t + c + 1, slice(c * H // 2, (c + 1) * H // 2)
                        sc = bs[:, c, :].rearrange("p (h k) -> p h k", h=H // 2)
                        after(dve, "a_s_ps", g, n)
                        V.tensor_reduce(mx1[:, hs], sc, AX_X, ALU.max).then_inc(S["a_max"], 1)
                        after(dve, "a_max", g, n)
                        V.tensor_tensor(p1[:, hs, :], sc, mx1[:, hs].unsqueeze(2).to_broadcast([P, H // 2, SEQ]),
                                        ALU.subtract).then_inc(S["a_sub"], 1)
                if s in (4, 9):
                    t = s // 9
                    for c in range(2):
                        hs = slice(c * H // 2, (c + 1) * H // 2)
                        after(dve, "a_p", g, 2 * t + c + 1)
                        V.tensor_reduce(sum1[:, hs], p1[:, hs, :], AX_X, ALU.add).then_inc(S["a_sum"], 1)
                    after(dve, "a_sum", g, 2 * t + 2)
                    V.reciprocal(ri1[:, :, :, :], sum1[:, :].rearrange("p (j h) -> p j h", h=2).unsqueeze(2)
                                 .to_broadcast([P, NJ, 2, 2])).then_inc(S["a_rinv"], 1)
                    after(dve, "a_rinv", g, t + 1)
                    if t == 1:
                        after(dve, "a_rT_ps", g, 1)
                    elif later(g):
                        after(dve, "a_rT_ps", g - 1, 2)
                    V.tensor_copy(rE[:, :, :], ri1[:, :, :, :].rearrange("p j n h -> p (j n h)").unsqueeze(2)
                                  .to_broadcast([P, 4 * NJ, DH])).then_inc(S["a_rE"], 1)
                if s in (7, 11):
                    t = s // 11
                    after(dve, "a_rT", g, t + 1)
                    after(dve, "a_y_ps", g, t + 1)
                    V.tensor_tensor(yT[:, :, :], bm[:, 0:2 * P].rearrange("p (m q) -> p m q", m=2), rT[:, :, :],
                                    ALU.mult).then_inc(S["a_y"], 1)
                if s in (8, 12):
                    t = s // 12
                    if t == 0:
                        after(dve, "a_xb", g, 1)
                        if later(g):
                            after(dve, "m_x2", g - 1, 1)
                    after(dve, "a_o_ps", g, t + 1)
                    V.tensor_tensor(x2[:, t, :], bm[:, 0:D], xb[:, t, :], ALU.add).then_inc(S["a_x2"], 1)

            def moe(g, s):
                if s == 0:
                    after(dve, "a_x2", g, TG)
                    norm("n4", x2, g)
                if s == 1:
                    norm_apply("n4", x2, g)
                if s == 2:
                    logits("m", g, bc[:, 1, :], 1, lg1, neg1, top1)
                    places("m", g, lg1, top1, idx1, idx1f, 1)
                    for t in range(TG):
                        V.tensor_scalar(oh1[:, t, :], iota[:, :], idx1f[:, t, :], None, ALU.is_equal)\
                         .then_inc(S["m_oh"], 1)
                    after(dve, "m_se", g, TG)
                    V.reciprocal(gate1[:, :], se1[:, :]).then_inc(S["m_gate"], 1)
                if s == 3:
                    after(dve, "m_oh", g, TG)
                    after(dve, "m_gate", g, 1)
                    after(dve, "m_c_ps", g, 1)
                    V.scalar_tensor_tensor(out=kw1[:, :, :], in0=bc[:, 0, 0:TG * E].rearrange("p (t e) -> p t e", t=TG),
                                           scalar=float(CAP), in1=oh1[:, :, :], op0=ALU.is_lt, op1=ALU.mult)\
                     .then_inc(S["m_kw"], 1)
                    V.tensor_tensor(macc[:, :], macc[:, :], oh1[:, 0, :], ALU.add).then_inc(S["m_macc"], 1)
                    V.tensor_scalar(gw1[:, :], gate1[:, :], tg[:, 3:4], None, ALU.mult).then_inc(S["m_gw"], 1)
                    after(dve, "m_macc", g, 1)
                    V.tensor_tensor(macc[:, :], macc[:, :], oh1[:, 1, :], ALU.add).then_inc(S["m_macc"], 1)
                if s in (11, 12):
                    t = s - 11
                    if t == 0:
                        after(dve, "m_x2", g, 1)
                        after(dve, "m_gw", g, 1)
                    after(dve, "m_e_ps", g, 2 * t + 2)
                    V.scalar_tensor_tensor(out=o_sb[:, t, :], in0=bc[:, t, 0:D], scalar=gw1[:, t:t + 1],
                                           in1=o_sb[:, t, :], op0=ALU.mult, op1=ALU.add).then_inc(S["m_out"], 1)

            run(dve, ORDER["vector"], front, attn, moe)

        @block.tensor
        def _(pe):
            def mm(dst, lhsT, rhs, start=True, stop=True, **kw):
                return nc.tensor.matmul(dst, lhsT, rhs, start=start, stop=stop, **kw)

            def turn(dst, src):
                n = src.partition_size()
                return nc.tensor.transpose(dst, src, ident[0:n, 0:n])

            pe.wait_ge(S["i_ident"], 1)
            pe.wait_ge(S["w_attn0"], 16 * 4)
            turn(bc[:, 0, 0:D], w0[:, 3, :])
            mm(bc[:, 0, D:2 * D], w0[:, 0, :], w0[:, 1, :])
            pe.wait_ge(S["w_cols0"], 16 * 2)
            mm(bc[:, 0, 2 * D:2 * D + 1], w0[:, 1, :], cols[:, 0:1]).then_inc(S["i_ps"], 1)
            pe.wait_ge(S["w_attn1"], 16 * 4)
            for n in range(4):
                last = turn(bs[:, 0, n * D:n * D + D], w1[:, n, :])
            last.then_inc(S["i_wps"], 1)
            pe.wait_ge(S["i_ev"], 1)
            pe.wait_ge(S["i_conv"], 4)
            mm(bc[:, 1, 0:D], w0[:, 2, :], woT[:, :])
            mm(bc[:, 1, D:2 * D], bv_bc[:, 0, :], woT[:, :]).then_inc(S["i_ps"], 1)

            def turn2(bank, src):
                for t in range(TG):
                    last = turn(bank[:, t * P:t * P + P], src[:, t, :])
                return last

            def front(g, s):
                if s == 0:
                    if later(g):
                        after(pe, "f_out", g - 1, 1)
                    after(pe, "ctx_loaded", g, 16)
                    turn2(fa, ctx_in).then_inc(S["f_ctxT_ps"], 1)
                if s == 1:
                    if isinstance(g, int) and g == 0:
                        pe.wait_ge(S["i_wev"], 1)
                    after(pe, "f_ctxT", g, 1)
                    mm(fa[:, 0:TG * P], w1T[:, 1, :], ctxT[:, :]).then_inc(S["a_k_ps"], 1)
                    after(pe, "n1_xn", g, TG)
                    turn2(fe[:, 0, :], xn["n1"]).then_inc(S["f_xnT_ps"], 1)
                if s == 2:
                    if isinstance(g, int) and g == 0:
                        pe.wait_ge(S["i_ev"], 5)
                    after(pe, "f_xnT", g, 1)
                    after(pe, "a_k", g, 1)
                    mm(fa[:, 0:TG * P], wqk[:, :], xnT[:, :]).then_inc(S["f_q_ps"], 1)
                    for t in range(TG):
                        last = mm(fe[:, 1, t * D:t * D + D], ctxT[:, t * P:t * P + P], wvo[:, :])
                    last.then_inc(S["f_v_ps"], 1)
                if s == 3:
                    after(pe, "f_q", g, 1)
                    for t in range(TG):
                        last = mm(fa[:, t * P:t * P + P], qT[:, t * P:t * P + P], ctxT[:, t * P:t * P + P])
                    last.then_inc(S["f_s_ps"], 1)
                if s == 4:
                    after(pe, "f_v", g, 1)
                    after(pe, "f_p", g, 2 * TG)
                    turn2(fe[:, 0, :], p0).then_inc(S["f_pT_ps"], 1)
                if s == 5:
                    after(pe, "f_pT", g, 1)
                    for t in range(TG):
                        last = mm(fa[:, t * D:t * D + D], p0T[:, t, :], vo[:, t, :])
                    last.then_inc(S["f_pv_ps"], 1)
                if s == 6:
                    after(pe, "n2_xn", g, TG)
                    turn2(fe[:, 0, :], xn["n2"]).then_inc(S["f_xn2T_ps"], 1)
                if s == 7:
                    after(pe, "f_xn2T", g, 1)
                    if isinstance(g, int) and g == 0:
                        pe.wait_ge(S["w_exp0"], 16 * 3)
                    for t in range(TG):
                        last = mm(fa[:, t * E:t * E + E], xn2T[:, t * P:t * P + P], w_e0[:, 0:E])
                    last.then_inc(S["f_r_ps"], 1)
                if 8 <= s < 8 + NU:
                    u = s - 8
                    if u >= 2:
                        after(pe, "f_chain", g, 4 * (u - 1))
                    elif later(g):
                        after(pe, "f_chain", g - 1, 4 * (u + 3))
                    for t in range(TG):
                        last = mm(fe[:, u % 2, 2 * t * D:2 * (t + 1) * D], xn2T[:, t * P:t * P + P],
                                  w_e0[:, E + 2 * u * D:E + 2 * (u + 1) * D])
                    last.then_inc(S["f_e_ps"], 1)
                if s == 10:
                    after(pe, "f_w", g, TG)
                    for t in range(TG):
                        last = turn(fa[0:E, t * P:t * P + P], w_tok0[:, t, :])
                    last.then_inc(S["f_wT_ps"], 1)
                if s == 12:
                    after(pe, "f_wT", g, 1)
                    for t in range(TG):
                        last = mm(fa[:, t * D:t * D + D], wT0[:, t * P:t * P + P], be0[:, :])
                    last.then_inc(S["f_b_ps"], 1)

            def attn(g, s):
                if s == 0:
                    if later(g):
                        after(pe, "a_x2", g - 1, TG)
                    else:
                        pe.wait_ge(S["i_conv"], 7)
                        for m in range(2):
                            turn(bm[:, m * D:m * D + D], wp_gap[:, m, :, :, :].rearrange("p j b c -> p (j b c)"))
                        pe.wait_ge(S["w_rows"], 16 * 5)
                        turn(bm[:, 2 * D:2 * D + E], b_up_rows[:, :]).then_inc(S["i_wps"], 1)
                        mm(bs[:, 1, 0:D], bv_bc[:, 1, :], w1T[:, 3, :]).then_inc(S["i_wps"], 1)
                        pe.wait_ge(S["i_bias"], 2)
                    for b in range(NB):
                        for h in range(2):
                            last = mm(bs[SEQ * h:SEQ * h + SEQ, 0, b * D:b * D + D], ctxT[:, b * SEQ:b * SEQ + SEQ],
                                      w1T[:, 2, :])
                    last.then_inc(S["a_v_ps"], 1)
                if s == 1:
                    after(pe, "n3_xn", g, TG)
                    turn2(bm, xn["n3"]).then_inc(S["a_xnT_ps"], 1)
                if s == 2:
                    after(pe, "a_xnT", g, 1)
                    mm(bm[:, 0:TG * P], w1T[:, 0, :], xn3T[:, :]).then_inc(S["a_q_ps"], 1)
                if s in (3, 6):
                    t = s // 6
                    if t == 0:
                        after(pe, "a_q", g, 1)
                        after(pe, "a_v", g, 2 * TG)
                    after(pe, "a_kx", g, 2 * t + 2)
                    for c in range(2):
                        if t == 1:
                            after(pe, "a_pT", g, c + 1)
                        for b in range(2):
                            q = t * P + b * SEQ
                            last = mm(bs[SEQ * b:SEQ * b + SEQ, c, :], q1T[:, q:q + SEQ],
                                      kx[:, 2 * t + b, (H // 2) * c:(H // 2) * (c + 1), :])
                        last.then_inc(S["a_s_ps"], 1)
                if s in (4, 9):
                    t = s // 9
                    for c in range(2):
                        after(pe, "a_p", g, 2 * t + c + 1)
                        for j in range(4):
                            last = turn(bs[:, c, j * P:j * P + P],
                                        p1[:, 8 * c + 2 * j:8 * c + 2 * j + 2, :].rearrange("p h k -> p (h k)"))
                        last.then_inc(S["a_pT_ps"], 1)
                if s in (5, 10):
                    t = s // 10
                    after(pe, "a_rE", g, t + 1)
                    if t == 1:
                        after(pe, "a_x2", g, 1)
                    for m in range(2):
                        last = turn(bm[:, m * P:m * P + P],
                                    rE[:, 2 * NJ * m:2 * NJ * (m + 1), :].rearrange("p n d -> p (n d)"))
                    last.then_inc(S["a_rT_ps"], 1)
                if s in (7, 11):
                    t = s // 11
                    after(pe, "a_rT", g, t + 1)
                    after(pe, "a_pT", g, 2 * t + 2)
                    for m in range(2):
                        for b in range(2):
                            for j in range(4):
                                v = (2 * (4 * m + j) + b) * 2 * DH
                                q = b * SEQ
                                last = mm(bm[32 * j:32 * j + 32, m * P + q:m * P + q + SEQ], vx[:, t, v:v + 4 * DH],
                                          p1T[:, 4 * m + j, q:q + SEQ], tile_position=(0, 32 * j))
                    last.then_inc(S["a_y_ps"], 1)
                if s in (8, 12):
                    t = s // 12
                    after(pe, "a_y", g, t + 1)
                    for m in range(2):
                        last = mm(bm[:, 0:D], yT[:, m, :], wpE[:, m, :], start=(m == 0), stop=(m == 1))
                    last.then_inc(S["a_o_ps"], 1)

            def moe(g, s):
                if s == 1:
                    if later(g):
                        after(pe, "m_out", g - 1, TG)
                    after(pe, "n4_xn", g, TG)
                    turn2(bc[:, 0, :], xn["n4"]).then_inc(S["m_xnT_ps"], 1)
                if s == 2:
                    if isinstance(g, int) and g == 0:
                        pe.wait_ge(S["w_exp1"], 16 * 4)
                    after(pe, "m_xnT", g, 1)
                    for t in range(TG):
                        last = mm(bc[:, 1, t * E:t * E + E], xn4T[:, t * P:t * P + P], w_r1[:, :])
                    last.then_inc(S["m_r_ps"], 1)
                if s == 3:
                    after(pe, "m_oh", g, TG)
                    if later(g):
                        after(pe, "m_macc", g - 1, 2)
                    mm(bc[:, 0, 0:E], tri[:, :], oh1[:, 0, :], stop=False)
                    mm(bc[:, 0, 0:E], ones_bf[:, :], macc[:, :], start=False)
                    mm(bc[:, 0, E:2 * E], tri[:, :], oh1[:, 1, :], stop=False)
                    mm(bc[:, 0, E:2 * E], ones_bf[:, :], oh1[:, 0, :], start=False, stop=False)
                    mm(bc[:, 0, E:2 * E], ones_bf[:, :], macc[:, :], start=False).then_inc(S["m_c_ps"], 1)
                if s == 4:
                    after(pe, "m_kw", g, 1)
                    for t in range(TG):
                        turn(bc[0:E, 1, (2 + t) * P:(3 + t) * P], kw1[:, t, :])
                    after(pe, "m_xg", g, TG)
                    turn2(bc[:, 1, :], xg).then_inc(S["m_xgT_ps"], 1)
                if 5 <= s < 5 + NU:
                    u = s - 5
                    if u == 0:
                        if isinstance(g, int) and g == 0:
                            pe.wait_ge(S["i_bar"], 1)
                        after(pe, "m_xgT", g, 1)
                    if u == 1:
                        after(pe, "m_kT", g, 1)
                    if u >= 2:
                        after(pe, "m_h", g, 2 * (u - 1))
                    for e in (2 * u, 2 * u + 1):
                        z = bc[:, u % 2, TG * P * (e % 2):TG * P * (e % 2 + 1)]
                        mm(z, w_up[:, e, :], xgT[:, :], stop=False)
                        if e == 0:
                            after(pe, "m_nT", g, 1)
                        last = mm(z, bar[:, e, :], nT1[:, :], start=False)
                    last.then_inc(S["m_h_ps"], 1)
                if 9 <= s < 13:
                    t, half = (s - 9) // 2, (s - 9) % 2
                    if s == 9:
                        after(pe, "m_h", g, E - 2)
                    if s == 10:
                        after(pe, "m_h", g, E)
                    z = bc[:, t, 0:D]
                    for e in range(4 * half, 4 * half + 4):
                        last = mm(z, hT[:, e, t * P:t * P + P], w_dn[:, e, :], start=(e == 0), stop=False)
                    if half == 1:
                        last = mm(z, kT1[:, t * P:t * P + P], be1[:, :], start=False)
                    last.then_inc(S["m_e_ps"], 1)

            run(pe, ORDER["tensor"], front, attn, moe)


_INS = ['x', 'ctx_1024', 'g_xattn', 'g_ffn', 'L0_xattn_Wk', 'L0_xattn_Wv', 'L0_xattn_bv', 'L0_xattn_Wq', 'L0_xattn_bq',
        'L0_xattn_Wo', 'L0_xattn_bo', 'L0_ffn_We', 'L0_ffn_be', 'L0_ffn_Wg', 'L0_ffn_bg', 'L1_xattn_Wq',
        'L1_xattn_bq', 'L1_xattn_Wk', 'L1_xattn_bk', 'L1_xattn_Wv', 'L1_xattn_bv', 'L1_xattn_Wp', 'L1_xattn_bp',
        'L1_ffn_Wr', 'L1_ffn_br', 'L1_ffn_W1', 'L1_ffn_b1', 'L1_ffn_W2', 'L1_ffn_b2']


def kernel(**inputs):
    import numpy as _np
    import concourse.bacc as _bacc
    from concourse import mybir as _mybir
    from concourse.bass_utils import run_bass_kernel_spmd as _run

    nc = _bacc.Bacc("TRN2", target_bir_lowering=False, num_devices=1)
    arrays, aps = {}, {}
    for name in _INS:
        v = _np.ascontiguousarray(inputs[name])
        arrays[f"in_{name}_dram"] = v
        aps[name] = nc.dram_tensor(f"in_{name}_dram", v.shape, _mybir.dt.from_np(v.dtype), kind="ExternalInput").ap()
    out = nc.dram_tensor("out_0_dram", inputs["x"].shape, _mybir.dt.float32, kind="ExternalOutput").ap()
    build_program(nc, aps, out)
    r = _run(nc, [arrays], core_ids=[0])
    return r.results[0]["out_0_dram"]
```
